# Optimizing a Trainium2 kernel written in Bass

```python
import numpy as np
import jax
import jax.numpy as jnp

def _softmax(x, axis=-1):
    return jax.nn.softmax(x, axis=axis)

def _gelu(x):
    return jax.nn.gelu(x, approximate=True)

def _silu(x):
    return jax.nn.silu(x)

def _sigmoid(x):
    return jax.nn.sigmoid(x)

def _layernorm(x, axis=-1, eps=1e-05):
    m = jnp.mean(x, axis=axis, keepdims=True)
    v = jnp.var(x, axis=axis, keepdims=True)
    return (x - m) / jnp.sqrt(v + eps)

def _scatter_add(tgt, idx, src, axis=0):
    return tgt.at[idx].add(src)

def _segment_sum(src, seg, n):
    return jax.ops.segment_sum(src, seg, n)
kernel_name = 'mk_decoder_postln_d2_seqx_r8_6c9b68'

def setup_inputs(seed: int=0):
    np.random.seed(seed)
    _w = jnp.asarray

    def _rec_inputs():
        import jax
        import jax.numpy as jnp
        _rk = jax.random.key(seed)
        x = 7.22e-05 + 1 * jax.random.normal(jax.random.fold_in(_rk, 1), (64, 128, 128), jnp.float32)
        _lenS = 128 - jax.random.randint(jax.random.fold_in(_rk, 7), (64,), 0, max(1, 128 // 4) + 1, jnp.int32)
        _lenS2 = 120 - jax.random.randint(jax.random.fold_in(_rk, 8), (64,), 0, max(1, 120 // 4) + 1, jnp.int32)
        fside_BxSxS_0 = 4.13588e-05 + 0.999923 * jax.random.normal(jax.random.fold_in(_rk, 11), (64, 128, 128), jnp.float32)
        _ctx_1024P = jax.random.normal(jax.random.fold_in(_rk, 12), (64, 16, 128), jnp.float32)
        _ctx_1024c = jax.random.dirichlet(jax.random.fold_in(_rk, 512), 0.3 * jnp.ones((16,), jnp.float32), (64, 120))
        _ctx_1024t = jnp.einsum('bsk,bkd->bsd', _ctx_1024c, _ctx_1024P)
        _ctx_1024t = _ctx_1024t * jax.lax.rsqrt(jnp.mean(jnp.square(_ctx_1024t)) + 1e-12) * 0.953939
        ctx_1024 = -0.000761806 + 0.999296 * (_ctx_1024t + 0.3 * jax.random.normal(jax.random.fold_in(_rk, 612), (64, 120, 128), jnp.float32))
        return (x, fside_BxSxS_0, ctx_1024)
    x, fside_BxSxS_0, ctx_1024 = _rec_inputs()

    def _L0_attn_setup():
        import jax, jax.numpy as jnp
        import numpy as np
        import math
        B, T, DIM = (4, 256, 128)
        N_HEADS, HEAD_DIM = (8, 128)
        WINDOW = 16
        EPS = 1e-06
        NEG = -1000000000.0

        def _alibi_slopes(n_heads):
            r = 2.0 ** (-8.0 / n_heads)
            return jnp.asarray([r ** i for i in range(n_heads)], dtype=jnp.float32)

        def _rms_norm(x, w, eps):
            var = jnp.mean(jnp.square(x), axis=-1, keepdims=True)
            return x * jax.lax.rsqrt(var + eps) * w
        key = jax.random.key(seed)
        ks = jax.random.split(key, 7)
        s = 1.0 / math.sqrt(DIM)
        return {'x': jax.random.normal(ks[0], (B, T, DIM), dtype=jnp.float32), 'wq': jax.random.normal(ks[1], (DIM, N_HEADS * HEAD_DIM), dtype=jnp.float32) * s, 'wk': jax.random.normal(ks[2], (DIM, N_HEADS * HEAD_DIM), dtype=jnp.float32) * s, 'wv': jax.random.normal(ks[3], (DIM, N_HEADS * HEAD_DIM), dtype=jnp.float32) * s, 'wo': jax.random.normal(ks[4], (N_HEADS * HEAD_DIM, DIM), dtype=jnp.float32) * s, 'q_norm_w': jnp.ones((N_HEADS * HEAD_DIM,), dtype=jnp.float32), 'k_norm_w': jnp.ones((N_HEADS * HEAD_DIM,), dtype=jnp.float32)}
    _L0_attn_all = _L0_attn_setup()
    _L0_attn_in = {k: v for k, v in _L0_attn_all.items() if k in ('wq', 'wk', 'wv', 'wo', 'q_norm_w', 'k_norm_w')}
    del _L0_attn_all

    def _L0_xattn_setup():
        import jax, jax.numpy as jnp
        import numpy as np
        DIM = 128
        HEADS = 16
        HEAD_DIM = DIM // HEADS
        B, N1, N2, SLOTS = (8, 128, 128, 64)
        key = jax.random.key(seed)
        ks = jax.random.split(key, 12)
        s = 1.0 / np.sqrt(DIM)
        return {'x1': jax.random.normal(ks[0], (B, N1, DIM), dtype=jnp.float32), 'x2': jax.random.normal(ks[1], (B, N2, DIM), dtype=jnp.float32), 'memory_k': jax.random.normal(ks[2], (B, SLOTS, DIM), dtype=jnp.float32), 'memory_v': jax.random.normal(ks[3], (B, SLOTS, DIM), dtype=jnp.float32), 'Wq': jax.random.normal(ks[4], (DIM, DIM), dtype=jnp.float32) * s, 'bq': jnp.zeros((DIM,), dtype=jnp.float32), 'Wk': jax.random.normal(ks[5], (DIM, DIM), dtype=jnp.float32) * s, 'bk': jnp.zeros((DIM,), dtype=jnp.float32), 'Wv': jax.random.normal(ks[6], (DIM, DIM), dtype=jnp.float32) * s, 'bv': jnp.zeros((DIM,), dtype=jnp.float32), 'Wp': jax.random.normal(ks[7], (DIM, DIM), dtype=jnp.float32) * s, 'bp': jnp.zeros((DIM,), dtype=jnp.float32)}
    _L0_xattn_all = _L0_xattn_setup()
    _L0_xattn_in = {k: v for k, v in _L0_xattn_all.items() if k in ('Wq', 'bq', 'Wk', 'bk', 'Wv', 'bv', 'Wp', 'bp')}
    del _L0_xattn_all

    def _L0_ffn_setup():
        import jax, jax.numpy as jnp
        import numpy as np
        EXPERTS = 8
        TOP_K = 2

        def swiglu(x, w1, w2, w3):
            h = x @ w1
            return h * jax.nn.sigmoid(h) * (x @ w2) @ w3
        key = jax.random.key(seed)
        ks = jax.random.split(key, 9)
        B, S, D = (4, 256, 128)
        H = 2 * D
        s = 0.02
        x = jax.random.normal(ks[0], (B, S, D), dtype=jnp.float32)
        gate_w = jax.random.normal(ks[1], (D, EXPERTS), dtype=jnp.float32) * s
        ew1 = jax.random.normal(ks[2], (EXPERTS, D, H), dtype=jnp.float32) * s
        ew2 = jax.random.normal(ks[3], (EXPERTS, D, H), dtype=jnp.float32) * s
        ew3 = jax.random.normal(ks[4], (EXPERTS, H, D), dtype=jnp.float32) * s
        sw1 = jax.random.normal(ks[5], (D, H), dtype=jnp.float32) * s
        sw2 = jax.random.normal(ks[6], (D, H), dtype=jnp.float32) * s
        sw3 = jax.random.normal(ks[7], (H, D), dtype=jnp.float32) * s
        return {'x': x, 'gate_w': gate_w, 'ew1': ew1, 'ew2': ew2, 'ew3': ew3, 'sw1': sw1, 'sw2': sw2, 'sw3': sw3}
    _L0_ffn_all = _L0_ffn_setup()
    _L0_ffn_in = {k: v for k, v in _L0_ffn_all.items() if k in ('gate_w', 'ew1', 'ew2', 'ew3', 'sw1', 'sw2', 'sw3')}
    del _L0_ffn_all

    def _L1_attn_setup():
        import jax, jax.numpy as jnp
        import numpy as np
        N_HEADS = 16
        ROPE_BASE = 10000.0

        def _rope_tables(seq_len, d_head, dtype):
            inv_freq = 1.0 / ROPE_BASE ** (jnp.arange(0, d_head, 2, dtype=jnp.float32) / d_head)
            t = jnp.arange(seq_len, dtype=jnp.float32)
            freqs = t[:, None] * inv_freq[None, :]
            return (jnp.cos(freqs).astype(dtype), jnp.sin(freqs).astype(dtype))

        def _apply_rope(x, cos, sin):
            half = x.shape[-1] // 2
            x1, x2 = (x[..., :half], x[..., half:])
            return jnp.concatenate([x1 * cos - x2 * sin, x2 * cos + x1 * sin], axis=-1)
        key = jax.random.key(seed)
        k1, k2, k3 = jax.random.split(key, 3)
        d_model = 128
        x = jax.random.normal(k1, (2, 256, d_model), dtype=jnp.float32)
        w_qkv = jax.random.normal(k2, (d_model, 3 * d_model), dtype=jnp.float32) * d_model ** (-0.5)
        w_out = jax.random.normal(k3, (d_model, d_model), dtype=jnp.float32) * d_model ** (-0.5)
        return {'x': x, 'w_qkv': w_qkv, 'w_out': w_out}
    _L1_attn_all = _L1_attn_setup()
    _L1_attn_in = {k: v for k, v in _L1_attn_all.items() if k in ('w_qkv', 'w_out')}
    del _L1_attn_all

    def _L1_xattn_setup():
        import jax, jax.numpy as jnp
        import numpy as np
        HEADS = 8
        DIM_HEAD = 64
        DIM = 128
        CTX_DIM = 128
        HIDDEN = HEADS * DIM_HEAD
        key = jax.random.key(seed)
        ks = jax.random.split(key, 7)
        b, n, m = (2, 256, 256)
        x = jax.random.normal(ks[0], (b, n, DIM), dtype=jnp.float32)
        context = jax.random.normal(ks[1], (b, m, CTX_DIM), dtype=jnp.float32)
        Wq = jax.random.normal(ks[2], (DIM, HIDDEN), dtype=jnp.float32) * (1.0 / np.sqrt(DIM))
        Wk = jax.random.normal(ks[3], (CTX_DIM, HIDDEN), dtype=jnp.float32) * (1.0 / np.sqrt(CTX_DIM))
        Wv = jax.random.normal(ks[4], (CTX_DIM, HIDDEN), dtype=jnp.float32) * (1.0 / np.sqrt(CTX_DIM))
        Wo = jax.random.normal(ks[5], (HIDDEN, DIM), dtype=jnp.float32) * (1.0 / np.sqrt(HIDDEN))
        bo = jax.random.normal(ks[6], (DIM,), dtype=jnp.float32) * 0.01
        return {'x': x, 'context': context, 'Wq': Wq, 'Wk': Wk, 'Wv': Wv, 'Wo': Wo, 'bo': bo}
    _L1_xattn_all = _L1_xattn_setup()
    _L1_xattn_in = {k: v for k, v in _L1_xattn_all.items() if k in ('Wq', 'Wk', 'Wv', 'Wo', 'bo')}
    del _L1_xattn_all

    def _L1_ffn_setup():
        import jax, jax.numpy as jnp
        import numpy as np
        HIDDEN = 128
        INNER = 512

        def _weight_quant(w):
            scale = 1.0 / jnp.clip(jnp.mean(jnp.abs(w)), 1e-05)
            wq = jnp.clip(jnp.round(w * scale), -1.0, 1.0) / scale
            return w + jax.lax.stop_gradient(wq - w)

        def _act_quant(x):
            scale = 127.0 / jnp.clip(jnp.max(jnp.abs(x), axis=-1, keepdims=True), 1e-05)
            xq = jnp.clip(jnp.round(x * scale), -128.0, 127.0) / scale
            return x + jax.lax.stop_gradient(xq - x)

        def _bitlinear(x, w):
            return jnp.einsum('bsi,oi->bso', _act_quant(x), _weight_quant(w))
        key = jax.random.key(seed)
        k0, k1, k2, k3 = jax.random.split(key, 4)
        x = jax.random.normal(k0, (4, 256, HIDDEN), dtype=jnp.float32)
        w_gate = jax.random.normal(k1, (INNER, HIDDEN), dtype=jnp.float32) / np.sqrt(HIDDEN)
        w_up = jax.random.normal(k2, (INNER, HIDDEN), dtype=jnp.float32) / np.sqrt(HIDDEN)
        w_down = jax.random.normal(k3, (HIDDEN, INNER), dtype=jnp.float32) / np.sqrt(INNER)
        return {'x': x, 'w_gate': w_gate, 'w_up': w_up, 'w_down': w_down}
    _L1_ffn_all = _L1_ffn_setup()
    _L1_ffn_in = {k: v for k, v in _L1_ffn_all.items() if k in ('w_gate', 'w_up', 'w_down')}
    del _L1_ffn_all
    return {'x': x, 'fside_BxSxS_0': fside_BxSxS_0, 'ctx_1024': ctx_1024, 'L0_attn_wq': _L0_attn_in['wq'], 'L0_attn_wk': _L0_attn_in['wk'], 'L0_attn_wv': _L0_attn_in['wv'], 'L0_attn_wo': _L0_attn_in['wo'], 'L0_attn_q_norm_w': _L0_attn_in['q_norm_w'], 'L0_attn_k_norm_w': _L0_attn_in['k_norm_w'], 'L0_xattn_Wq': _L0_xattn_in['Wq'], 'L0_xattn_bq': _L0_xattn_in['bq'], 'L0_xattn_Wk': _L0_xattn_in['Wk'], 'L0_xattn_bk': _L0_xattn_in['bk'], 'L0_xattn_Wv': _L0_xattn_in['Wv'], 'L0_xattn_bv': _L0_xattn_in['bv'], 'L0_xattn_Wp': _L0_xattn_in['Wp'], 'L0_xattn_bp': _L0_xattn_in['bp'], 'L0_ffn_gate_w': _L0_ffn_in['gate_w'], 'L0_ffn_ew1': _L0_ffn_in['ew1'], 'L0_ffn_ew2': _L0_ffn_in['ew2'], 'L0_ffn_ew3': _L0_ffn_in['ew3'], 'L0_ffn_sw1': _L0_ffn_in['sw1'], 'L0_ffn_sw2': _L0_ffn_in['sw2'], 'L0_ffn_sw3': _L0_ffn_in['sw3'], 'L1_attn_w_qkv': _L1_attn_in['w_qkv'], 'L1_attn_w_out': _L1_attn_in['w_out'], 'L1_xattn_Wq': _L1_xattn_in['Wq'], 'L1_xattn_Wk': _L1_xattn_in['Wk'], 'L1_xattn_Wv': _L1_xattn_in['Wv'], 'L1_xattn_Wo': _L1_xattn_in['Wo'], 'L1_xattn_bo': _L1_xattn_in['bo'], 'L1_ffn_w_gate': _L1_ffn_in['w_gate'], 'L1_ffn_w_up': _L1_ffn_in['w_up'], 'L1_ffn_w_down': _L1_ffn_in['w_down']}

def reference(x, fside_BxSxS_0, ctx_1024, L0_attn_wq, L0_attn_wk, L0_attn_wv, L0_attn_wo, L0_attn_q_norm_w, L0_attn_k_norm_w, L0_xattn_Wq, L0_xattn_bq, L0_xattn_Wk, L0_xattn_bk, L0_xattn_Wv, L0_xattn_bv, L0_xattn_Wp, L0_xattn_bp, L0_ffn_gate_w, L0_ffn_ew1, L0_ffn_ew2, L0_ffn_ew3, L0_ffn_sw1, L0_ffn_sw2, L0_ffn_sw3, L1_attn_w_qkv, L1_attn_w_out, L1_xattn_Wq, L1_xattn_Wk, L1_xattn_Wv, L1_xattn_Wo, L1_xattn_bo, L1_ffn_w_gate, L1_ffn_w_up, L1_ffn_w_down):
    import jax
    import jax.numpy as jnp

    def _L0_attn_ref(x, wq, wk, wv, wo, q_norm_w, k_norm_w):
        import jax, jax.numpy as jnp
        import numpy as np
        import math
        B, T, DIM = (4, 256, 128)
        N_HEADS, HEAD_DIM = (8, 128)
        WINDOW = 16
        EPS = 1e-06
        NEG = -1000000000.0

        def _alibi_slopes(n_heads):
            r = 2.0 ** (-8.0 / n_heads)
            return jnp.asarray([r ** i for i in range(n_heads)], dtype=jnp.float32)

        def _rms_norm(x, w, eps):
            var = jnp.mean(jnp.square(x), axis=-1, keepdims=True)
            return x * jax.lax.rsqrt(var + eps) * w
        Bx, Tx, _ = x.shape
        xq = _rms_norm(x @ wq, q_norm_w, EPS)
        xk = _rms_norm(x @ wk, k_norm_w, EPS)
        xv = x @ wv
        q = xq.reshape(Bx, Tx, N_HEADS, HEAD_DIM).transpose(0, 2, 1, 3)
        k = xk.reshape(Bx, Tx, N_HEADS, HEAD_DIM).transpose(0, 2, 1, 3)
        v = xv.reshape(Bx, Tx, N_HEADS, HEAD_DIM).transpose(0, 2, 1, 3)
        pos = jnp.arange(Tx)
        rel = pos[None, :] - pos[:, None]
        slopes = _alibi_slopes(N_HEADS)
        bias = slopes[:, None, None] * rel.astype(jnp.float32)
        invalid = (rel > 0) | (rel < -WINDOW)
        bias = jnp.where(invalid[None, :, :], NEG, bias)
        scale = 1.0 / math.sqrt(HEAD_DIM)
        scores = jnp.einsum('bhqd,bhkd->bhqk', q, k) * scale + bias[None]
        probs = jax.nn.softmax(scores, axis=-1)
        y = jnp.einsum('bhqk,bhkd->bhqd', probs, v)
        y = y.transpose(0, 2, 1, 3).reshape(Bx, Tx, N_HEADS * HEAD_DIM)
        return y @ wo

    def _L0_xattn_ref(x1, x2, memory_k, memory_v, Wq, bq, Wk, bk, Wv, bv, Wp, bp):
        import jax, jax.numpy as jnp
        import numpy as np
        DIM = 128
        HEADS = 16
        HEAD_DIM = DIM // HEADS
        B, N1, N2, SLOTS = (8, 128, 128, 64)
        Bn, Nq, C = x1.shape
        H, D = (HEADS, HEAD_DIM)
        scale = D ** (-0.5)
        q = (x1 @ Wq + bq).reshape(Bn, Nq, H, D).transpose(0, 2, 1, 3)
        k = x2 @ Wk + bk
        v = x2 @ Wv + bv
        k = jnp.concatenate([k, memory_k], axis=1)
        v = jnp.concatenate([v, memory_v], axis=1)
        Nkv = k.shape[1]
        k = k.reshape(Bn, Nkv, H, D).transpose(0, 2, 1, 3)
        v = v.reshape(Bn, Nkv, H, D).transpose(0, 2, 1, 3)
        attn = jnp.einsum('bhqd,bhkd->bhqk', q, k) * scale
        attn = jax.nn.softmax(attn, axis=-1)
        out = jnp.einsum('bhqk,bhkd->bhqd', attn, v)
        out = out.transpose(0, 2, 1, 3).reshape(Bn, Nq, C)
        return out @ Wp + bp

    def _L0_ffn_ref(x, gate_w, ew1, ew2, ew3, sw1, sw2, sw3):
        import jax, jax.numpy as jnp
        import numpy as np
        EXPERTS = 8
        TOP_K = 2

        def swiglu(x, w1, w2, w3):
            h = x @ w1
            return h * jax.nn.sigmoid(h) * (x @ w2) @ w3
        B, S, D = x.shape
        gate_out = x @ gate_w
        top_v, top_i = jax.lax.top_k(gate_out, TOP_K)
        masked = jnp.full_like(gate_out, -1e+20)
        bi = jnp.arange(B)[:, None, None]
        si = jnp.arange(S)[None, :, None]
        masked = masked.at[bi, si, top_i].set(top_v)
        probs = jax.nn.softmax(masked, axis=-1)
        chosen = jnp.zeros_like(gate_out, dtype=bool).at[bi, si, top_i].set(True)
        w = jnp.where(chosen, probs, 0.0)

        def one_expert(w1, w2, w3, we):
            return swiglu(x, w1, w2, w3) * we[..., None]
        out = jax.vmap(one_expert, in_axes=(0, 0, 0, 2))(ew1, ew2, ew3, w).sum(0)
        out = out + swiglu(x, sw1, sw2, sw3)
        return out

    def _L1_attn_ref(x, w_qkv, w_out):
        import jax, jax.numpy as jnp
        import numpy as np
        N_HEADS = 16
        ROPE_BASE = 10000.0

        def _rope_tables(seq_len, d_head, dtype):
            inv_freq = 1.0 / ROPE_BASE ** (jnp.arange(0, d_head, 2, dtype=jnp.float32) / d_head)
            t = jnp.arange(seq_len, dtype=jnp.float32)
            freqs = t[:, None] * inv_freq[None, :]
            return (jnp.cos(freqs).astype(dtype), jnp.sin(freqs).astype(dtype))

        def _apply_rope(x, cos, sin):
            half = x.shape[-1] // 2
            x1, x2 = (x[..., :half], x[..., half:])
            return jnp.concatenate([x1 * cos - x2 * sin, x2 * cos + x1 * sin], axis=-1)
        B, S, D = x.shape
        H = N_HEADS
        dh = D // H
        scale = dh ** (-0.5)
        qkv = x @ w_qkv
        q, k, v = jnp.split(qkv, 3, axis=-1)

        def to_heads(t):
            return t.reshape(B, S, H, dh).transpose(0, 2, 1, 3)
        q, k, v = (to_heads(q), to_heads(k), to_heads(v))
        cos, sin = _rope_tables(S, dh, x.dtype)
        q = _apply_rope(q, cos, sin)
        k = _apply_rope(k, cos, sin)
        scores = jnp.einsum('bhqd,bhkd->bhqk', q, k) * scale
        causal = jnp.tril(jnp.ones((S, S), dtype=bool))
        scores = jnp.where(causal, scores, jnp.finfo(scores.dtype).min)
        attn = jax.nn.softmax(scores, axis=-1)
        out = jnp.einsum('bhqk,bhkd->bhqd', attn, v)
        out = out.transpose(0, 2, 1, 3).reshape(B, S, D)
        return out @ w_out

    def _L1_xattn_ref(x, context, Wq, Wk, Wv, Wo, bo):
        import jax, jax.numpy as jnp
        import numpy as np
        HEADS = 8
        DIM_HEAD = 64
        DIM = 128
        CTX_DIM = 128
        HIDDEN = HEADS * DIM_HEAD
        b, n, _ = x.shape
        m = context.shape[1]
        scale = DIM_HEAD ** (-0.5)
        q = (x @ Wq).reshape(b, n, HEADS, DIM_HEAD).transpose(0, 2, 1, 3)
        k = (context @ Wk).reshape(b, m, HEADS, DIM_HEAD).transpose(0, 2, 1, 3)
        v = (context @ Wv).reshape(b, m, HEADS, DIM_HEAD).transpose(0, 2, 1, 3)
        scores = jnp.einsum('bhnd,bhmd->bhnm', q, k) * scale
        attn = jax.nn.softmax(scores, axis=-1)
        out = jnp.einsum('bhnm,bhmd->bhnd', attn, v)
        out = out.transpose(0, 2, 1, 3).reshape(b, n, HIDDEN)
        return out @ Wo + bo

    def _L1_ffn_ref(x, w_gate, w_up, w_down):
        import jax, jax.numpy as jnp
        import numpy as np
        HIDDEN = 128
        INNER = 512

        def _weight_quant(w):
            scale = 1.0 / jnp.clip(jnp.mean(jnp.abs(w)), 1e-05)
            wq = jnp.clip(jnp.round(w * scale), -1.0, 1.0) / scale
            return w + jax.lax.stop_gradient(wq - w)

        def _act_quant(x):
            scale = 127.0 / jnp.clip(jnp.max(jnp.abs(x), axis=-1, keepdims=True), 1e-05)
            xq = jnp.clip(jnp.round(x * scale), -128.0, 127.0) / scale
            return x + jax.lax.stop_gradient(xq - x)

        def _bitlinear(x, w):
            return jnp.einsum('bsi,oi->bso', _act_quant(x), _weight_quant(w))
        gate = jax.nn.silu(_bitlinear(x, w_gate))
        up = _bitlinear(x, w_up)
        return _bitlinear(gate * up, w_down)
    x = _layernorm(x + _L0_attn_ref(x, L0_attn_wq, L0_attn_wk, L0_attn_wv, L0_attn_wo, L0_attn_q_norm_w, L0_attn_k_norm_w), axis=-1)
    x = _layernorm(x + _L0_xattn_ref(x, fside_BxSxS_0, ctx_1024, ctx_1024, L0_xattn_Wq, L0_xattn_bq, L0_xattn_Wk, L0_xattn_bk, L0_xattn_Wv, L0_xattn_bv, L0_xattn_Wp, L0_xattn_bp), axis=-1)
    x = _layernorm(x + _L0_ffn_ref(x, L0_ffn_gate_w, L0_ffn_ew1, L0_ffn_ew2, L0_ffn_ew3, L0_ffn_sw1, L0_ffn_sw2, L0_ffn_sw3), axis=-1)
    x = _layernorm(x + _L1_attn_ref(x, L1_attn_w_qkv, L1_attn_w_out), axis=-1)
    x = _layernorm(x + _L1_xattn_ref(x, ctx_1024, L1_xattn_Wq, L1_xattn_Wk, L1_xattn_Wv, L1_xattn_Wo, L1_xattn_bo), axis=-1)
    x = _layernorm(x + _L1_ffn_ref(x, L1_ffn_w_gate, L1_ffn_w_up, L1_ffn_w_down), axis=-1)
    return x

_drawn_inputs = setup_inputs


def setup_inputs(seed=0):
    import zlib

    import numpy as np

    out = dict(_drawn_inputs(seed))
    spreads = {'L0_attn_q_norm_w': (1.0, 0.2),
     'L0_attn_k_norm_w': (1.0, 0.2),
     'L0_xattn_bq': (0.0, 0.29),
     'L0_xattn_bk': (0.0, 0.557),
     'L0_xattn_bv': (0.0, 0.1),
     'L0_xattn_bp': (0.0, 0.1)}
    factors = {'L0_ffn_gate_w': 8.0,
     'L0_ffn_ew1': 8.0,
     'L0_ffn_ew2': 8.0,
     'L0_ffn_ew3': 8.0,
     'L0_ffn_sw1': 7.18,
     'L0_ffn_sw2': 7.098,
     'L0_ffn_sw3': 7.081,
     'L1_xattn_bo': 5.717}
    for name, (base, spread) in spreads.items():
        noise = np.random.default_rng([zlib.crc32(name.encode()), seed]).standard_normal(out[name].shape)
        drawn = base * np.exp(spread * noise) if base else spread * noise
        out[name] = jnp.asarray(drawn.astype(out[name].dtype))
    for name, factor in factors.items():
        out[name] = (out[name] * factor).astype(out[name].dtype)
    return out
```

```python
from contextlib import ExitStack

import numpy as np
import concourse.bass as bass
from concourse import mybir

F32 = mybir.dt.float32
BF16 = mybir.dt.bfloat16
U32 = mybir.dt.uint32
ALU = mybir.AluOpType
ACT = mybir.ActivationFunctionType
AX = mybir.AxisListType

P = 128
CTX = 120
WH = 8
NH = 16
HD = P // NH
EXPERTS = 8
HID = 256
INNER = 512
LN_EPS = 1e-5
RMS_EPS = 1e-6
ROUND = 1.5 * 2.0 ** 23


class At:

    def __init__(self, p, r, ring, count):
        self.p = p + r // ring if r // ring else p
        self.slot, self.ring, self.count = r % ring, ring, count

    def __add__(self, k):
        return At(self.p, self.slot + k, self.ring, self.count)

    def __sub__(self, k):
        return self + (-k)

    @property
    def n(self):
        return self.p * self.ring + self.slot if self.slot else self.p * self.ring

    @property
    def live(self):
        return not isinstance(self.p, int) or 0 <= self.n < self.count

    def done(self, per=1, part=None):
        return self.p * (self.ring * per) + (self.slot * per + (per if part is None else part))

    def landed(self):
        return self.p * 16 + 16


def need(eng, sem, value):
    if not isinstance(value, int) or value > 0:
        eng.wait_ge(sem, value)


def pipeline(eng, step, ring, count, first, lo, hi, last):
    for i in range(first, lo):
        step(At(i // ring, i % ring, ring, count))
    with eng.Fori(lo // ring, hi // ring) as p:
        for r in range(ring):
            step(At(p, r, ring, count))
    for i in range(hi, last):
        step(At(i // ring, i % ring, ring, count))


class Core:

    def __init__(self, nc, ctx):
        self.nc, self.ctx, self.taken, self.signals = nc, ctx, 0, []
        self.small = self.sb("small", [P, 512])

    def sb(self, name, shape, dtype=F32, ctx=None):
        count = int(np.prod(shape[1:]))
        if ctx is None or count >= 64 or dtype == U32:
            return (ctx or self.ctx).enter_context(self.nc.sbuf_tensor(name, shape, dtype))
        part = self.small[:, self.taken:self.taken + count]
        self.taken += count
        return part if len(shape) == 2 else part.rearrange("p (a b) -> p a b", a=shape[1])

    def sem(self, name, ctx):
        self.signals.append(ctx.enter_context(self.nc.semaphore(name)))
        return self.signals[-1]

    def clear(self):
        with self.nc.Block() as block:
            @block.sync
            def _(sp):
                for s in self.signals:
                    sp.sem_clear(s)
        self.signals.clear()


def allocate(K):
    K.S = [K.ctx.enter_context(K.nc.psum_tensor(f"psS{i}", [P, 1024], F32)) for i in range(2)]
    K.W = [K.ctx.enter_context(K.nc.psum_tensor(f"psW{i}", [P, 512], F32)) for i in range(4)]
    K.pr = [K.sb(f"pr{i}", [P, 1024]) for i in range(4)]
    K.ident = K.sb("ident", [P, P])
    K.identb = K.sb("identb", [P, P], BF16)
    K.alibi = K.sb("alibi", [P, WH * P])
    K.causal = K.sb("causal", [P, 4 * P], BF16)
    K.headmask = K.sb("headmask", [P, NH])
    K.rope = K.sb("rope", [P, 4 * P])
    K.unround = K.sb("unround", [P, 1])
    K.half = K.sb("half", [P, 2])
    K.eps = K.sb("eps", [P, 1])
    K.Mself = K.sb("Mself", [P, WH * P])
    K.Nself = K.sb("Nself", [P, WH * P])
    K.Gram = K.sb("Gram", [P, 2 * P])
    K.Mcross = K.sb("Mcross", [P, WH * P])
    K.Ncross = K.sb("Ncross", [P, WH * P])
    K.xw = K.sb("xw", [P, 4, P])
    K.xb = K.sb("xb", [P, 2])
    K.rowb = K.sb("rowb", [P, 3, P])
    K.rw = K.sb("rw", [P, 6, P])
    K.gate = K.sb("gate", [P, EXPERTS])
    K.e1 = K.sb("e1", [P, EXPERTS + 1, HID])
    K.e2 = K.sb("e2", [P, EXPERTS + 1, HID])
    K.e3 = K.sb("e3", [P, EXPERTS + 1, 2, P])
    K.tg = K.sb("tg", [P, INNER], BF16)
    K.tu = K.sb("tu", [P, INNER], BF16)
    K.td = K.sb("td", [P, 4, P], BF16)
    K.tmean = K.sb("tmean", [P, 3])
    K.tstep = K.sb("tstep", [P, 3])
    K.iota = K.sb("iota", [P, EXPERTS])


def set_up(K, D):
    nc = K.nc
    with ExitStack() as ctx:
        stage = K.sb("stage", [P, 3, WH * P], F32, ctx)
        stage2 = K.sb("stage2", [P, 3, 512], F32, ctx)
        wo = K.sb("wo", [P, WH, P], F32, ctx)
        wo2 = K.sb("wo2", [P, 4, P], F32, ctx)
        qkw = K.sb("qkw", [P, 2, WH], F32, ctx)
        qk = K.sb("qk", [P, WH], F32, ctx)
        wT = K.sb("wT", [P, 3, WH * P], F32, ctx)
        wTs = K.sb("wTs", [P, WH * P], F32, ctx)
        wT2 = K.sb("wT2", [P, 3, 512], F32, ctx)
        tern = K.sb("tern", [P, 3, 4, P], F32, ctx)
        ternq = K.sb("ternq", [P, 3, 4, P], F32, ctx)
        tabs = K.sb("tabs", [P, 3], F32, ctx)
        tsc = K.sb("tsc", [P, 3], F32, ctx)
        ones = K.sb("ones", [P, P], F32, ctx)
        w_in = K.sem("w_in", ctx)
        causal = K.sb("causal_in", [P, P], F32, ctx)
        made = K.sem("made", ctx)
        halved = K.sem("halved", ctx)
        pe_done = K.sem("pe_done", ctx)
        taken = K.sem("taken", ctx)
        banks = [K.S[0][:, 0:512], K.S[0][:, 512:1024], K.S[1][:, 0:512], K.S[1][:, 512:1024]] + [w[:] for w in K.W]

        loads = [
            (K.ident[:], D["c_ident"]), (K.alibi[:], D["c_alibi"]),
            (causal[:], D["c_causal"]), (K.headmask[:], D["c_headmask"]), (K.rope[:], D["c_rope"]), (K.iota[:], D["c_iota"]),
            (stage[:, 0, :], D["L0_attn_wq"]), (stage[:, 1, :], D["L0_attn_wk"]), (stage[:, 2, :], D["L0_attn_wv"]),
            (wo[:], D["L0_attn_wo"].rearrange("(h e) n -> e h n", e=P)),
            (qkw[:, 0, :], D["L0_attn_q_norm_w"].rearrange("(h e) -> e h", e=P)),
            (qkw[:, 1, :], D["L0_attn_k_norm_w"].rearrange("(h e) -> e h", e=P)),
            (stage2[:, 0, :], D["L1_xattn_Wq"]), (stage2[:, 1, :], D["L1_xattn_Wk"]), (stage2[:, 2, :], D["L1_xattn_Wv"]),
            (wo2[:], D["L1_xattn_Wo"].rearrange("(b e) n -> e b n", e=P)),
            (K.xw[:, 0, :], D["L0_xattn_Wq"]), (K.xw[:, 1, :], D["L0_xattn_Wk"]),
            (K.xw[:, 2, :], D["L0_xattn_Wv"]), (K.xw[:, 3, :], D["L0_xattn_Wp"]),
            (K.xb[:, 0:1], D["L0_xattn_bq"].rearrange("(d a) -> d a", a=1)),
            (K.xb[:, 1:2], D["L0_xattn_bk"].rearrange("(d a) -> d a", a=1)),
            (K.rowb[:, 0, :], D["L0_xattn_bv"].rearrange("(a d) -> a d", a=1).to_broadcast([P, P])),
            (K.rowb[:, 1, :], D["L0_xattn_bp"].rearrange("(a d) -> a d", a=1).to_broadcast([P, P])),
            (K.rowb[:, 2, :], D["L1_xattn_bo"].rearrange("(a d) -> a d", a=1).to_broadcast([P, P])),
            (K.rw[:, 0:3, :], D["L1_attn_w_qkv"].rearrange("d (t n) -> d t n", t=3)),
            (K.rw[:, 5, :], D["L1_attn_w_out"]),
            (K.gate[:], D["L0_ffn_gate_w"]),
            (K.e1[:, 0:EXPERTS, :], D["L0_ffn_ew1"].rearrange("e d f -> d e f")), (K.e1[:, EXPERTS, :], D["L0_ffn_sw1"]),
            (K.e2[:, 0:EXPERTS, :], D["L0_ffn_ew2"].rearrange("e d f -> d e f")), (K.e2[:, EXPERTS, :], D["L0_ffn_sw2"]),
            (K.e3[:, 0:EXPERTS, :, :], D["L0_ffn_ew3"].rearrange("e (b f) n -> f e b n", b=2)),
            (K.e3[:, EXPERTS, :, :], D["L0_ffn_sw3"].rearrange("(b f) n -> f b n", b=2)),
            (tern[:, 0, :, :], D["L1_ffn_w_gate"].rearrange("(b o) i -> o b i", b=4)),
            (tern[:, 1, :, :], D["L1_ffn_w_up"].rearrange("(b o) i -> o b i", b=4)),
            (tern[:, 2, :, :], D["L1_ffn_w_down"].rearrange("o (b i) -> o b i", b=4)),
        ]
        LOADED = 16 * len(loads)

        turns = []
        for t in range(3):
            for g in range(2):
                turns.append(([stage[:, t, (4 * g + j) * P:(4 * g + j + 1) * P] for j in range(4)],
                              wT[:, t, 512 * g:512 * g + 512]))
        for t in range(3):
            turns.append(([stage2[:, t, j * P:(j + 1) * P] for j in range(4)], wT2[:, t, :]))
        first_turns = len(turns)
        late = [([ternq[:, t, j, :] for j in range(4)], dst)
                for t, dst in ((0, K.tg[:]), (1, K.tu[:]), (2, K.td[:].rearrange("p b n -> p (b n)")))]

        def products():
            cols = lambda j: slice(j * P, (j + 1) * P)
            for g in range(2):
                h = [4 * g + j for j in range(4)]
                yield [(cols(j), wTs[:, cols(h[j])], wT[:, 1, cols(h[j])], True, True) for j in range(4)], \
                    K.Mself[:, 512 * g:512 * g + 512]
                yield [(cols(j), wT[:, 2, cols(h[j])], wo[:, h[j], :], True, True) for j in range(4)], \
                    K.Nself[:, 512 * g:512 * g + 512]
                row = lambda k: slice(64 * (k % 2), 64 * (k % 2) + 64)
                wide = lambda t: t[:].rearrange("p (j a n) -> p j a n", a=2, n=P)[:, :, g, :]
                yield [(cols(j), wT2[row(g), 0, cols(j)], wT2[row(g), 1, cols(j)], True, True) for j in range(4)], \
                    wide(K.Mcross)
                yield [(cols(j), wT2[row(g), 2, cols(j)], wo2[row(g), j, :], True, True) for j in range(4)], \
                    wide(K.Ncross)
            yield [(cols(t), wT[:, t, cols(h)], wT[:, t, cols(h)], h == 0, h == WH - 1)
                   for t in range(2) for h in range(WH)], K.Gram[:]

        made_list = list(products())

        with nc.Block() as block:
            @block.sync
            def _(sp):
                for dst, src in loads:
                    sp.dma_start(dst, src, allow_slow_non_contiguous=True).then_inc(w_in, 16)

            @block.gpsimd
            def _(pool):
                pool.memset(K.half[:], -0.5).then_inc(halved, 1)
                pool.memset(K.eps[:], LN_EPS).then_inc(halved, 1)
                pool.memset(K.unround[:], -ROUND).then_inc(halved, 1)
                pool.wait_ge(halved, 3)

            @block.vector
            def _(dve):
                dve.memset(ones[:], 1.0).then_inc(made, 1)
                dve.wait_ge(w_in, LOADED)
                for h in range(4):
                    dve.tensor_copy(K.causal[:, h * P:(h + 1) * P], causal[:])
                dve.tensor_copy(K.identb[:], K.ident[:]).then_inc(made, 1)
                dve.tensor_tensor(qk[:], qkw[:, 0, :], qkw[:, 1, :], ALU.mult).then_inc(made, 1)
                for t in range(3):
                    dve.tensor_reduce(tabs[:, t:t + 1], tern[:, t, :, :].rearrange("p b i -> p (b i)"), AX.X,
                                      ALU.add, apply_absolute_value=True).then_inc(made, 1)
                for t in range(2):
                    w = K.rw[:, t, :].rearrange("p (h a d) -> p h a d", h=NH, a=2)
                    r = K.rw[:, 3 + t, :].rearrange("p (h a d) -> p h a d", h=NH, a=2)
                    dve.tensor_scalar(r[:, :, 0, :], w[:, :, 1, :], -1.0, None, ALU.mult).then_inc(made, 1)
                    dve.tensor_copy(r[:, :, 1, :], w[:, :, 0, :]).then_inc(made, 1)
                dve.wait_ge(made, 3)
                dve.wait_ge(taken, 2)
                for h in range(WH):
                    dve.tensor_scalar(wTs[:, h * P:(h + 1) * P], wT[:, 0, h * P:(h + 1) * P], qk[:, h:h + 1], None,
                                      ALU.mult).then_inc(made, 1)
                dve.wait_ge(pe_done, first_turns + 1)
                dve.tensor_scalar(K.tmean[:], banks[first_turns % 8][:, 0:3], 1.0 / (INNER * P), 1e-5, ALU.mult,
                                  ALU.max).then_inc(made, 1)
                dve.wait_ge(made, 19)
                dve.reciprocal(tsc[:], K.tmean[:]).then_inc(made, 1)
                dve.wait_ge(made, 20)
                for t in range(3):
                    dve.tensor_scalar(ternq[:, t, :, :], tern[:, t, :, :], tsc[:, t:t + 1], ROUND, ALU.mult,
                                      ALU.add).then_inc(made, 1)
                dve.wait_ge(made, 23)
                for t in range(3):
                    dve.tensor_scalar(ternq[:, t, :, :], ternq[:, t, :, :], ROUND, 1.0, ALU.subtract,
                                      ALU.min).then_inc(made, 1)
                dve.wait_ge(made, 26)
                for t in range(3):
                    dve.tensor_scalar(ternq[:, t, :, :], ternq[:, t, :, :], -1.0, None, ALU.max).then_inc(made, 1)
                dve.tensor_scalar(K.tstep[:, 0:1], K.tmean[:, 0:1], 0.5, None, ALU.mult).then_inc(made, 1)
                dve.tensor_scalar(K.tstep[:, 2:3], K.tmean[:, 2:3], 1.0 / 127.0, None, ALU.mult).then_inc(made, 1)

            @block.tensor
            def _(pe):
                pe.wait_ge(w_in, LOADED)
                n = 0
                for srcs, _ in turns:
                    if n >= 8:
                        pe.wait_ge(taken, n - 7)
                    for j, src in enumerate(srcs):
                        last = pe.transpose(banks[n % 8][:, j * P:(j + 1) * P], src, K.ident[:])
                    last.then_inc(pe_done, 1)
                    n += 1
                pe.wait_ge(made, 6)
                pe.wait_ge(taken, n - 7)
                pe.matmul(banks[n % 8][:, 0:3], ones[:], tabs[:], start=True, stop=True).then_inc(pe_done, 1)
                n += 1
                pe.wait_ge(made, 18)
                pe.wait_ge(taken, first_turns)
                for mms, _ in made_list:
                    pe.wait_ge(taken, n - 7)
                    for c, lhsT, rhs, start, stop in mms:
                        last = pe.matmul(banks[n % 8][:, c], lhsT, rhs, start=start, stop=stop)
                    last.then_inc(pe_done, 1)
                    n += 1
                pe.wait_ge(made, 29)
                for srcs, _ in late:
                    pe.wait_ge(taken, n - 7)
                    for j, src in enumerate(srcs):
                        last = pe.transpose(banks[n % 8][:, j * P:(j + 1) * P], src, K.ident[:])
                    last.then_inc(pe_done, 1)
                    n += 1

            @block.scalar
            def _(act):
                n = 0
                for _, dst in turns:
                    act.wait_ge(pe_done, n + 1)
                    act.copy(dst, banks[n % 8][:]).then_inc(taken, 1)
                    n += 1
                act.wait_ge(made, 19)
                act.drain().then_inc(taken, 1)
                n += 1
                for mms, dst in made_list + late:
                    act.wait_ge(pe_done, n + 1)
                    src = banks[n % 8]
                    src = src.rearrange("p (j n) -> p j n", n=P) if len(dst.shape) == 3 else src[:, 0:dst.shape[1]]
                    act.copy(dst, src).then_inc(taken, 1)
                    n += 1
        K.clear()


def attend_wide(K, D, tag, x_dram, out_dram, nseq, windowed):
    nc = K.nc
    ring = 4
    keys = P if windowed else CTX
    M, N = (K.Mself, K.Nself) if windowed else (K.Mcross, K.Ncross)
    last_gain = P ** -0.5 if windowed else 64 ** -0.5
    K.taken = 0
    with ExitStack() as ctx:
        def sb(name, shape, dtype=F32):
            return K.sb(tag + name, shape, dtype, ctx)

        def sem(name):
            return K.sem(tag + name, ctx)

        x = [sb(f"x{i}", [P, P]) for i in range(ring)]
        cx = [sb(f"cx{i}", [P, P]) for i in range(ring)]
        res = [sb(f"res{i}", [P, P]) for i in range(ring)]
        xT = [sb(f"xT{i}", [P, P]) for i in range(ring)]
        xs = [sb(f"xs{i}", [P, 2 * P]) for i in range(2)]
        sT = [sb(f"sT{i}", [P, 2 * P]) for i in range(ring)]
        junk = sb("junk", [P, P])
        ss = [sb(f"ss{i}", [P, 2]) for i in range(2)]
        rms = [sb(f"rms{i}", [P, 2]) for i in range(2)]
        xM = [sb(f"xM{i}", [P, WH * P]) for i in range(2)]
        U = [sb(f"U{i}", [P, WH * P]) for i in range(ring)]
        pr = K.pr
        nmax = [sb(f"nmax{i}", [P, WH]) for i in range(2)]
        tot = [sb(f"tot{i}", [P, WH]) for i in range(ring)]
        inv = [sb(f"inv{i}", [P, WH]) for i in range(ring)]
        pT = [sb(f"pT{i}", [P, WH * P]) for i in range(2)]
        y = [sb(f"y{i}", [P, P]) for i in range(2)]
        yb = sb("yb", [P, P])
        stats = [sb(f"st{i}", [P, 6]) for i in range(2)]
        mv = [sb(f"mv{i}", [P, 2]) for i in range(2)]
        ve = [sb(f"ve{i}", [P, 1]) for i in range(2)]
        rs = [sb(f"rs{i}", [P, 1]) for i in range(2)]
        xo = [sb(f"xo{i}", [P, P]) for i in range(ring)]

        x_in = [sem(f"x_in{i}") for i in range(ring)]
        cx_in = [sem(f"cx_in{i}") for i in range(ring)]
        res_in = [sem(f"res_in{i}") for i in range(ring)]
        stored = [sem(f"stored{i}") for i in range(ring)]
        xT_ps, sT_ps, gram_ps, xM_ps = sem("xT_ps"), sem("sT_ps"), sem("gram_ps"), sem("xM_ps")
        S_ps, U_ps, pT_ps, out_ps = sem("S_ps"), sem("U_ps"), sem("pT_ps"), sem("out_ps")
        xM_sb, U_sb, exped = sem("xM_sb"), sem("U_sb"), sem("exped")
        xT_sb, sT_sb, pT_sb, squared, scaled = sem("xT_sb"), sem("sT_sb"), sem("pT_sb"), sem("squared"), sem("scaled")
        biased, maxed, inverted, summed = sem("biased"), sem("maxed"), sem("inverted"), sem("summed")
        counted, meaned, normed = sem("counted"), sem("meaned"), sem("normed")
        joined = sem("joined")
        rooted, eased, lnroot, weighed = sem("rooted"), sem("eased"), sem("lnroot"), sem("weighed")

        W = K.W
        span = (-5, 8, (nseq - 5) // ring * ring, nseq + 6)

        with nc.Block() as block:
            @block.sync
            def _(sp):
                def step(c):
                    a = c + 5
                    if a.live:
                        need(sp, scaled if windowed else xT_ps, (a - 4).done(2 if windowed else 1))
                        sp.dma_start(x[a.slot][:], x_dram[a.n]).then_inc(x_in[a.slot], 16)
                        if not windowed:
                            sp.dma_start(cx[a.slot][0:CTX, :], D["ctx_1024"][a.n]).then_inc(cx_in[a.slot], 16)
                    if c.live:
                        need(sp, summed, (c - 4).done())
                        sp.dma_start(res[c.slot][:], x_dram[c.n]).then_inc(res_in[c.slot], 16)
                    o = c - 5
                    if o.live:
                        need(sp, normed, o.done())
                        sp.dma_start(out_dram[o.n], xo[o.slot][:]).then_inc(stored[o.slot], 16)
                pipeline(sp, step, ring, nseq, *span)
                for i in range(ring):
                    sp.wait_ge(stored[i], 16 * len(range(i, nseq, ring)))

            @block.tensor
            def _(pe):
                def step(c):
                    t, m, g, b, a = c - 3, c + 1, c + 2, c, c + 3
                    if t.live:
                        need(pe, weighed, t.done(2))
                        if (c + 1).live and windowed:
                            need(pe, squared, (c + 1).done(2))
                        need(pe, pT_sb, (t - 1).done(2))
                        need(pe, U_sb, (c - 1).done(2) if (c - 1).live else 0)
                        for half in range(2):
                            for j in range(4):
                                h = 4 * half + j
                                last = pe.transpose(W[half][0:keys, j * P:(j + 1) * P],
                                                    pr[t.slot][:, h * P:h * P + keys], K.ident[:])
                            last.then_inc(pT_ps, 1)
                    if m.live:
                        if windowed:
                            need(pe, sT_sb, m.done())
                        need(pe, xT_sb, (c + 2).done() if (c + 2).live else m.done())
                        need(pe, summed, (t - 1).done())
                        for half in range(2):
                            for j in range(4):
                                h = 4 * half + j
                                last = pe.matmul(W[2 + half][:, j * P:(j + 1) * P], M[:, h * P:(h + 1) * P],
                                                 sT[m.slot][:, 0:P] if windowed else xT[m.slot][:],
                                                 start=True, stop=True)
                            last.then_inc(xM_ps, 1)
                    if g.live and windowed:
                        need(pe, xT_sb, g.done())
                        need(pe, pT_sb, t.done(2, 1))
                        pe.matmul(W[0][:, 0:2 * P], xT[g.slot][:], K.Gram[:], start=True, stop=True).then_inc(gram_ps, 1)
                    if b.live:
                        need(pe, xM_sb, b.done(2))
                        need(pe, maxed if not windowed else biased, (b - 2).done())
                        if not windowed:
                            need(pe, exped, (b - 2).done(2))
                        for h in range(WH):
                            last = pe.matmul(K.S[b.slot % 2][:, h * P:h * P + keys], xM[b.slot % 2][:, h * P:(h + 1) * P],
                                             sT[b.slot][:, P:P + keys], start=True, stop=True)
                        last.then_inc(S_ps, 1)
                        need(pe, pT_sb, t.done(2))
                        if m.live:
                            need(pe, xM_sb, m.done(2, 1))
                        for half in range(2):
                            pe.matmul(W[1 + half][0:keys, :], (xT[b.slot][:] if windowed else sT[b.slot][:, P:P + keys]),
                                      N[:, 512 * half:512 * half + 512], start=True, stop=True).then_inc(U_ps, 1)
                    if t.live:
                        need(pe, pT_sb, t.done(2))
                        need(pe, U_sb, t.done(2))
                        if m.live:
                            need(pe, xM_sb, m.done(2))
                        need(pe, summed, (t - 1).done())
                        for h in range(WH):
                            last = pe.matmul(W[3][:, 0:P], pT[t.slot % 2][0:keys, h * P:(h + 1) * P],
                                             U[t.slot][0:keys, h * P:(h + 1) * P], start=(h == 0), stop=(h == WH - 1))
                        last.then_inc(out_ps, 1)
                    if b.live:
                        need(pe, U_sb, b.done(2))
                    elif m.live:
                        need(pe, xM_sb, m.done(2))
                    if g.live and windowed:
                        need(pe, scaled, g.done(2))
                        pe.transpose(W[2][:, P:2 * P], xs[g.slot % 2][:, 0:P], K.ident[:])
                        pe.transpose(W[2][:, 2 * P:3 * P], xs[g.slot % 2][:, P:2 * P], K.ident[:]).then_inc(sT_ps, 1)
                    if a.live:
                        if not b.live:
                            need(pe, xT_sb, (a - 1).done())
                        need(pe, x_in[a.slot], a.landed())
                        last = pe.transpose(W[2][:, 0:P], x[a.slot][:], K.ident[:])
                        if not windowed:
                            need(pe, cx_in[a.slot], a.landed())
                            last = pe.transpose(W[2][:, P:P + CTX], cx[a.slot][0:CTX, :], K.ident[0:CTX, 0:CTX])
                        last.then_inc(xT_ps, 1)
                pipeline(pe, step, ring, nseq, *span)

            @block.scalar
            def _(act):
                def step(c):
                    m, e, b = c + 1, c - 1, c
                    if m.live:
                        for half in range(2):
                            need(act, xM_ps, m.done(2, half + 1))
                            need(act, S_ps, (m - 2).done())
                            act.activation(xM[m.slot % 2][:, 512 * half:512 * half + 512], W[2 + half][:], ACT.Copy,
                                           scale=1.0 if windowed else last_gain).then_inc(xM_sb, 1)
                    if e.live:
                        need(act, maxed, e.done())
                        need(act, inverted, (e - 4).done())
                        need(act, pT_ps, (e - 4).done(2))
                        src = pr[e.slot] if windowed else K.S[e.slot % 2]
                        for h in range(WH):
                            last = act.activation(pr[e.slot][:, h * P:h * P + keys], src[:, h * P:h * P + keys], ACT.Exp,
                                                  bias=nmax[e.slot % 2][:, h:h + 1], accum_out=tot[e.slot][:, h:h + 1])
                            if h % 4 == 3:
                                last.then_inc(exped, 1)
                    if b.live:
                        need(act, out_ps, (b - 4).done())
                        for half in range(2):
                            need(act, U_ps, b.done(2, half + 1))
                            act.copy(U[b.slot][0:keys, 512 * half:512 * half + 512], W[1 + half][0:keys, :]).then_inc(U_sb, 1)
                pipeline(act, step, ring, nseq, *span)

            @block.vector
            def _(dve):
                def step(c):
                    t, n, g, b, e, a = c - 3, c - 4, c + 2, c, c - 1, c + 3
                    if t.live:
                        need(dve, out_ps, (t - 2).done())
                        for half in range(2):
                            need(dve, pT_ps, t.done(2, half + 1))
                            dve.tensor_copy(pT[t.slot % 2][0:keys, 512 * half:512 * half + 512],
                                            W[half][0:keys, :]).then_inc(pT_sb, 1)
                    if n.live:
                        dve.wait_ge(lnroot, n.done())
                        need(dve, stored[n.slot], (n - 4).landed())
                        dve.tensor_scalar(xo[n.slot][:], y[n.slot % 2][:], mv[n.slot % 2][:, 0:1], rs[n.slot % 2][:, 0:1],
                                          ALU.subtract, ALU.mult).then_inc(normed, 1)
                    if g.live and windowed:
                        dve.wait_ge(gram_ps, g.done())
                        need(dve, rooted, (g - 2).done())
                        for k in range(2):
                            if k == 1:
                                dve.wait_ge(squared, g.done(2, 1))
                            else:
                                need(dve, squared, (g - 1).done(2))
                            dve.tensor_tensor_reduce(out=junk[:], in0=W[0][:, k * P:(k + 1) * P], in1=x[g.slot][:],
                                                     scale=1.0 / (WH * P), scalar=RMS_EPS, op0=ALU.mult, op1=ALU.add,
                                                     accum_out=ss[g.slot % 2][:, k:k + 1]).then_inc(squared, 1)
                    if b.live:
                        dve.wait_ge(S_ps, b.done())
                        src = K.S[b.slot % 2][:]
                        need(dve, exped, (b - 2).done(2))
                        if windowed:
                            need(dve, pT_ps, (b - 4).done(2))
                            dve.tensor_tensor(pr[b.slot][:], K.S[b.slot % 2][:], K.alibi[:], ALU.add).then_inc(biased, 1)
                            src = pr[b.slot][:]
                            dve.wait_ge(biased, b.done())
                        dve.tensor_reduce(nmax[b.slot % 2][:], src.rearrange("p (h k) -> p h k", h=WH)[:, :, 0:keys],
                                          AX.X, ALU.max, negate=True).then_inc(maxed, 1)
                    if g.live and windowed:
                        dve.wait_ge(rooted, g.done())
                        need(dve, sT_ps, (g - 2).done())
                        dve.tensor_scalar(xs[g.slot % 2][:, 0:P], x[g.slot][:], rms[g.slot % 2][:, 0:1], last_gain,
                                          ALU.mult, ALU.mult).then_inc(scaled, 1)
                        dve.tensor_scalar(xs[g.slot % 2][:, P:2 * P], x[g.slot][:], rms[g.slot % 2][:, 1:2], None,
                                          ALU.mult).then_inc(scaled, 1)
                    if e.live:
                        dve.wait_ge(exped, e.done(2))
                        need(dve, weighed, (e - 4).done(2))
                        dve.reciprocal(inv[e.slot][:], tot[e.slot][:]).then_inc(inverted, 1)
                    if t.live:
                        dve.wait_ge(res_in[t.slot], t.landed())
                        need(dve, normed, (t - 2).done())
                        if not windowed:
                            dve.tensor_tensor(yb[:], res[t.slot][:], K.rowb[:, 2, :], ALU.add).then_inc(joined, 1)
                            dve.wait_ge(joined, t.done())
                        dve.wait_ge(out_ps, t.done())
                        dve.tensor_tensor(y[t.slot % 2][:], W[3][:, 0:P], (res[t.slot] if windowed else yb)[:],
                                          ALU.add).then_inc(summed, 1)
                        dve.wait_ge(summed, t.done())
                        dve.bn_stats(stats[t.slot % 2][:], y[t.slot % 2][:]).then_inc(counted, 1)
                    if g.live and windowed:
                        dve.wait_ge(sT_ps, g.done())
                        if a.live:
                            dve.wait_ge(xT_ps, a.done())
                        need(dve, S_ps, (g - 4).done())
                        dve.tensor_copy(sT[g.slot][:], W[2][:, P:3 * P]).then_inc(sT_sb, 1)
                    if a.live:
                        dve.wait_ge(xT_ps, a.done())
                        need(dve, U_ps, (a - 4).done(2))
                        if not windowed:
                            need(dve, S_ps, (a - 4).done())
                            dve.tensor_copy(sT[a.slot][:, P:P + CTX], W[2][:, P:P + CTX])
                        if t.live:
                            dve.wait_ge(counted, t.done())
                        dve.tensor_copy(xT[a.slot][:], W[2][:, 0:P]).then_inc(xT_sb, 1)
                    if t.live:
                        dve.wait_ge(counted, t.done()) if not a.live else None
                        dve.bn_aggr(mv[t.slot % 2][:], stats[t.slot % 2][:]).then_inc(meaned, 1)
                pipeline(dve, step, ring, nseq, *span)

            @block.gpsimd
            def _(pool):
                def weigh(w, half):
                    for h in range(4 * half, 4 * half + 4):
                        last = pool.tensor_scalar(pr[w.slot][:, h * P:h * P + keys], pr[w.slot][:, h * P:h * P + keys],
                                                  inv[w.slot][:, h:h + 1], 1.0, ALU.mult, ALU.mult)
                    last.then_inc(weighed, 1)

                def step(c):
                    n, w, g = c - 4, c - 2, c + 2
                    if w.live:
                        pool.wait_ge(inverted, w.done())
                    if n.live:
                        pool.wait_ge(meaned, n.done())
                        need(pool, lnroot, (n - 1).done())
                        need(pool, normed, (n - 2).done())
                        pool.tensor_tensor(ve[n.slot % 2][:], mv[n.slot % 2][:, 1:2], K.eps[:], ALU.add).then_inc(eased, 1)
                        pool.wait_ge(eased, n.done())
                        pool.tensor_tensor(rs[n.slot % 2][:], ve[n.slot % 2][:], K.half[:, 0:1], ALU.pow).then_inc(lnroot, 1)
                    if w.live:
                        weigh(w, 0)
                    if g.live and windowed:
                        pool.wait_ge(squared, g.done(2))
                        need(pool, scaled, (g - 2).done(2))
                        pool.tensor_tensor(rms[g.slot % 2][:], ss[g.slot % 2][:], K.half[:], ALU.pow).then_inc(rooted, 1)
                    if w.live:
                        weigh(w, 1)
                pipeline(pool, step, ring, nseq, *span)
        K.clear()


def attend_narrow(K, D, tag, x_dram, out_dram, nseq, cross):
    nc = K.nc
    units = 4 if cross else 2
    ring, uring, ucount = 4, 4 * units, nseq * units
    per_unit = NH // units
    wide = 1024 // per_unit
    keys = P + CTX if cross else P
    chunks = [(0, P), (P, CTX)] if cross else [(0, P)]
    behind = 1 if cross else 2
    gain = HD ** -0.5

    def heads(j):
        return [4 * g + m for m in range(j * per_unit // 4, (j + 1) * per_unit // 4) for g in range(4)]

    def item(u):
        return At(u.p, u.slot // units, ring, nseq)

    def bank(x):
        return not isinstance(x.p, int) or 0 <= x.n < nseq + 2 + behind

    K.taken = 0
    with ExitStack() as ctx:
        def sb(name, shape, dtype=F32):
            return K.sb(tag + name, shape, dtype, ctx)

        def sem(name):
            return K.sem(tag + name, ctx)

        x = [sb(f"x{i}", [P, P]) for i in range(ring)]
        fs = [sb(f"fs{i}", [P, P]) for i in range(ring)] if cross else None
        cx = [sb(f"cx{i}", [P, P]) for i in range(ring)] if cross else None
        res = [sb(f"res{i}", [P, P]) for i in range(ring)]
        xT = [sb(f"xT{i}", [P, 2 * P]) for i in range(ring)]
        qk = [sb(f"qk{i}", [P, P + keys]) for i in range(ring)]
        spun = [sb(f"spun{i}", [P, 2 * P]) for i in range(2)]
        Qx = [sb(f"Qx{i}", [P, NH, P]) for i in range(2)]
        Vx = [sb(f"Vx{i}", [P, len(chunks), NH, 32]) for i in range(ring)]
        pr = K.pr
        nmax = [sb(f"nmax{i}", [P, per_unit]) for i in range(4)]
        tot = [sb(f"tot{i}", [P, NH]) for i in range(ring)]
        inv = [sb(f"inv{i}", [P, NH]) for i in range(2)]
        invx = [sb(f"invx{i}", [P, P]) for i in range(2)]
        invT = [sb(f"invT{i}", [P, P]) for i in range(2)]
        oT = [sb(f"oT{i}", [P, P]) for i in range(2)]
        pT = [sb(f"pT{i}", [P, 1024]) for i in range(2)]
        y = [sb(f"y{i}", [P, P]) for i in range(2)]
        yb = [sb(f"yb{i}", [P, P]) for i in range(2)]
        stats = [sb(f"st{i}", [P, 6]) for i in range(2)]
        mv = [sb(f"mv{i}", [P, 2]) for i in range(2)]
        ve = [sb(f"ve{i}", [P, 1]) for i in range(2)]
        rs = [sb(f"rs{i}", [P, 1]) for i in range(2)]
        xo = [sb(f"xo{i}", [P, P]) for i in range(ring)]
        junk = sb("junk", [P, 1])

        x_in = [sem(f"x_in{i}") for i in range(ring)]
        res_in = [sem(f"res_in{i}") for i in range(ring)]
        stored = [sem(f"stored{i}") for i in range(ring)]
        shared_ps, proj_ps, S_ps, pT_ps, O_ps, inv_ps = (sem(n) for n in (
            "shared_ps", "proj_ps", "S_ps", "pT_ps", "O_ps", "inv_ps"))
        shared_sb, proj_sb, invT_sb, oT_sb = (sem(n) for n in ("shared_sb", "proj_sb", "invT_sb", "oT_sb"))
        pT_sb = [sem("pT_sb0"), sem("pT_sb1")]
        exped, halves, maxed, inverted, spread = (sem(n) for n in (
            "exped", "halves", "maxed", "inverted", "spread"))
        joined, summed, counted, meaned, normed = (sem(n) for n in ("joined", "summed", "counted", "meaned", "normed"))
        cleared, masked, eased, lnroot = sem("cleared"), sem("masked"), sem("eased"), sem("lnroot")

        W = K.W
        arrivals = 3 if cross else 1
        span = (-2 * units, ring * units, (nseq - 3) // ring * ring * units, (nseq + behind + 2) * units)
        wq, wk, wv, wout = (K.xw[:, n, :] for n in range(4)) if cross else (K.rw[:, n, :] for n in (0, 1, 2, 5))

        def turn(t, half, copy):
            cols = slice(512 * half, 512 * half + 512)
            if not cross:
                return copy(pT[t.slot % 2][:, cols], W[half][:])
            w = W[half][:].rearrange("p (n c q) -> p n c q", n=2, c=2)
            d = pT[t.slot % 2][:, cols].rearrange("p (n c q) -> p n c q", n=2, c=2)
            copy(d[:, :, 0, :], w[:, :, 0, :])
            return copy(d[0:CTX, :, 1, :], w[0:CTX, :, 1, :])

        with nc.Block() as block:
            @block.sync
            def _(sp):
                def step(c):
                    a, o = c + 4, c - 4
                    if a.live:
                        need(sp, proj_sb, (a - 4).done())
                        sp.dma_start(x[a.slot][:], x_dram[a.n]).then_inc(x_in[a.slot], 16)
                        if cross:
                            sp.dma_start(fs[a.slot][:], D["fside_BxSxS_0"][a.n]).then_inc(x_in[a.slot], 16)
                            sp.dma_start(cx[a.slot][0:CTX, :], D["ctx_1024"][a.n]).then_inc(x_in[a.slot], 16)
                    if c.live:
                        need(sp, summed, (c - 4).done())
                        sp.dma_start(res[c.slot][:], x_dram[c.n]).then_inc(res_in[c.slot], 16)
                    if o.live:
                        need(sp, normed, o.done())
                        sp.dma_start(out_dram[o.n], xo[o.slot][:]).then_inc(stored[o.slot], 16)
                pipeline(sp, step, ring, nseq, -4, 4, (nseq - 4) // ring * ring, nseq + 4)
                for i in range(ring):
                    sp.wait_ge(stored[i], 16 * len(range(i, nseq, ring)))

            @block.tensor
            def _(pe):
                pe.wait_ge(cleared, ring)

                def step(u):
                    t, j, i = u - 2, u.slot % units, item(u)
                    b, a = i + 1, i + 2
                    if t.live:
                        need(pe, exped, t.done())
                        for half in range(2):
                            need(pe, pT_sb[half], (t - 1).done())
                            for n in range(4 * half, 4 * half + 4):
                                at, size = (wide * (n // 2) + chunks[n % 2][0], chunks[n % 2][1]) if cross else (n * P, P)
                                last = pe.transpose(W[half][0:size, (n % 4) * P:(n % 4 + 1) * P],
                                                    pr[t.slot % 4][:, at:at + size], K.ident[:])
                            last.then_inc(pT_ps, 1)
                    if j == 0 and b.live:
                        need(pe, shared_sb, b.done())
                        if cross:
                            pe.matmul(W[2][:, 0:P], wq, xT[b.slot][:, 0:P], start=True, stop=True)
                            pe.matmul(W[2][:, P:2 * P], wk, xT[b.slot][:, P:2 * P], start=True, stop=True)
                            last = pe.matmul(W[2][:, 2 * P:3 * P], xT[b.slot][:, P:2 * P], wv, start=True, stop=True)
                        else:
                            for n, w in enumerate((wq, wk, K.rw[:, 3, :], K.rw[:, 4, :])):
                                last = pe.matmul(W[2][:, n * P:(n + 1) * P], w, xT[b.slot][:, 0:P], start=True, stop=True)
                        last.then_inc(proj_ps, 1)
                    r = u - 3
                    if r.live and r.slot % units == units - 1:
                        k = item(r)
                        need(pe, spread, k.done())
                        pe.transpose(W[3][:, P:2 * P], invx[k.slot % 2][:], K.ident[:]).then_inc(inv_ps, 1)
                    if j == units - 1 and bank(a):
                        o = i + (-behind)
                        last = None
                        if b.live:
                            need(pe, proj_sb, b.done())
                        else:
                            need(pe, shared_sb, (a - 1).done())
                        if o.live:
                            need(pe, oT_sb, o.done())
                            last = pe.matmul(W[2][:, 0:P], oT[o.slot % 2][:], wout, start=True, stop=True)
                        if not cross and b.live:
                            last = pe.matmul(W[2][:, P:2 * P], xT[b.slot][:, 0:P], wv, start=True, stop=True)
                        if a.live:
                            need(pe, x_in[a.slot], a.p * (16 * arrivals) + 16 * arrivals)
                            if cross:
                                pe.transpose(W[2][:, 2 * P:3 * P], fs[a.slot][:], K.ident[:])
                                pe.transpose(W[2][:, 3 * P:3 * P + CTX], cx[a.slot][0:CTX, :], K.ident[0:CTX, 0:CTX])
                                last = pe.transpose(W[2][:, P:2 * P], x[a.slot][:], K.ident[:])
                            else:
                                last = pe.transpose(W[2][:, 2 * P:3 * P], x[a.slot][:], K.ident[:])
                        last.then_inc(shared_ps, 1)
                    if u.live:
                        need(pe, masked, u.done())
                        need(pe, exped, (u - 2).done())
                        if not cross:
                            for half in range(2):
                                pe.matmul(K.S[u.slot % 2][:, 512 * half:512 * half + 512], K.identb[:], K.causal[:],
                                          start=True, stop=False)
                        for n, h in enumerate(heads(j)):
                            last = pe.matmul(K.S[u.slot % 2][:, n * wide:n * wide + keys], Qx[i.slot % 2][:, h, :],
                                             qk[i.slot][:, P:P + keys], start=cross,
                                             stop=cross or n % 4 == 3)
                        last.then_inc(S_ps, 1)
                    if t.live:
                        k, tj = item(t), t.slot % units
                        need(pe, pT_sb[0], t.done())
                        need(pe, pT_sb[1], t.done())
                        need(pe, oT_sb, (k - 1).done())
                        for n in range(8):
                            h, c = (heads(tj)[n // 2], n % 2) if cross else (heads(tj)[n], 0)
                            first = tj == 0 and (n % 2 == 0 if cross else n < 4)
                            final = tj == units - 1 and (n % 2 == 1 if cross else n >= 4)
                            size = chunks[c][1]
                            g = h // 4
                            last = pe.matmul(W[3][32 * g:32 * g + 32, 0:P], Vx[k.slot][0:size, c, h, :],
                                             pT[t.slot % 2][0:size, n * P:(n + 1) * P], start=first, stop=final)
                        last.then_inc(O_ps, 1)
                pipeline(pe, step, uring, ucount, *span)

            @block.scalar
            def _(act):
                def step(u):
                    e, t = u - 1, u - 2
                    if t.live:
                        need(act, O_ps, (t - 2).done())
                        need(act, pT_ps, t.done(2))
                        turn(t, 1, act.copy).then_inc(pT_sb[1], 1)
                    if e.live:
                        need(act, maxed, e.done())
                        need(act, pT_ps, (e - 4).done(2))
                        k = item(e)
                        need(act, inverted, (k - 4).done())
                        for n, h in enumerate(heads(e.slot % units)):
                            cols = slice(n * wide, n * wide + keys)
                            last = act.activation(pr[e.slot % 4][:, cols], K.S[e.slot % 2][:, cols], ACT.Exp,
                                                  bias=nmax[e.slot % 4][:, n:n + 1], accum_out=tot[k.slot][:, h:h + 1])
                        last.then_inc(exped, 1)
                pipeline(act, step, uring, ucount, *span)

            @block.vector
            def _(dve):
                for i in range(ring):
                    dve.memset(Vx[i][:], 0.0).then_inc(cleared, 1)
                dve.wait_ge(cleared, ring)

                def put(slot, c, size, src, bias):
                    v = Vx[slot][0:size, c, :, :]
                    for m in range(4):
                        dst = v[:, m:NH:4, HD * m:HD * m + HD]
                        s = src.rearrange("p (g m d) -> p m g d", g=4, m=4)[:, m]
                        if bias is None:
                            last = dve.tensor_copy(dst, s)
                        else:
                            last = dve.tensor_tensor(dst, s, bias.rearrange("p (g m d) -> p m g d", g=4, m=4)[:, m], ALU.add)
                    return last

                def step(u):
                    t, j, i = u - 2, u.slot % units, item(u)
                    b, a = i + 1, i + 2
                    if t.live:
                        need(dve, O_ps, (t - 2).done())
                        need(dve, pT_ps, t.done(2, 1))
                        turn(t, 0, dve.tensor_copy).then_inc(pT_sb[0], 1)
                    if j == 0:
                        if b.live:
                            need(dve, proj_ps, b.done())
                            need(dve, S_ps, (b - 4).done(units))
                            need(dve, masked, (b - 4).done(units))
                            if cross:
                                dve.tensor_scalar(qk[b.slot][:, 0:P], W[2][:, 0:P], K.xb[:, 0:1], gain, ALU.add, ALU.mult)
                                dve.tensor_scalar(qk[b.slot][:, P:2 * P], W[2][:, P:2 * P], K.xb[:, 1:2], None, ALU.add)
                                need(dve, O_ps, (b - 4).done(units))
                                put(b.slot, 1, CTX, cx[b.slot][0:CTX, :], None)
                                put(b.slot, 0, P, W[2][:, 2 * P:3 * P], K.rowb[:, 0, :]).then_inc(proj_sb, 1)
                            else:
                                for s in range(2):
                                    dve.tensor_tensor(spun[s][:], W[2][:, 2 * s * P:2 * (s + 1) * P],
                                                      K.rope[:, 2 * s * P:2 * (s + 1) * P], ALU.mult).then_inc(halves, 1)
                                dve.wait_ge(halves, b.done(2))
                                dve.tensor_tensor(qk[b.slot][:], spun[0][:], spun[1][:], ALU.add).then_inc(proj_sb, 1)
                    r = u - 3
                    if r.live and r.slot % units == units - 1:
                        k = item(r)
                        need(dve, inv_ps, k.done())
                        dve.tensor_copy(invT[k.slot % 2][:], W[3][:, P:2 * P]).then_inc(invT_sb, 1)
                        need(dve, shared_ps, (k + behind).done())
                        need(dve, invT_sb, k.done())
                        dve.tensor_tensor(oT[k.slot % 2][:], W[3][:, 0:P], invT[k.slot % 2][:], ALU.mult).then_inc(oT_sb, 1)
                    if j == units - 1 and bank(a):
                        need(dve, shared_ps, a.done())
                        o = i + (-behind)
                        if o.live:
                            need(dve, res_in[o.slot], o.landed())
                            need(dve, normed, (o - 2).done())
                            if cross:
                                dve.tensor_tensor(yb[o.slot % 2][:], res[o.slot][:], K.rowb[:, 1, :], ALU.add).then_inc(joined, 1)
                                need(dve, joined, o.done())
                            dve.tensor_tensor(y[o.slot % 2][:], W[2][:, 0:P], (yb[o.slot % 2] if cross else res[o.slot])[:],
                                              ALU.add).then_inc(summed, 1)
                            need(dve, summed, o.done())
                            dve.bn_stats(stats[o.slot % 2][:], y[o.slot % 2][:]).then_inc(counted, 1)
                        if not cross and b.live:
                            need(dve, O_ps, (b - 4).done(units))
                            put(b.slot, 0, P, W[2][:, P:2 * P], None)
                        if o.live:
                            need(dve, counted, o.done())
                        if a.live:
                            if cross:
                                need(dve, S_ps, (a - 4).done(units))
                                dve.tensor_copy(qk[a.slot][:, 2 * P:2 * P + CTX], W[2][:, 3 * P:3 * P + CTX])
                                dve.tensor_copy(xT[a.slot][:], W[2][:, P:3 * P]).then_inc(shared_sb, 1)
                            else:
                                dve.tensor_copy(xT[a.slot][:, 0:P], W[2][:, 2 * P:3 * P]).then_inc(shared_sb, 1)
                        else:
                            dve.tensor_copy(junk[:], K.half[:, 0:1]).then_inc(shared_sb, 1)
                        if o.live:
                            dve.bn_aggr(mv[o.slot % 2][:], stats[o.slot % 2][:]).then_inc(meaned, 1)
                    if u.live:
                        need(dve, S_ps, u.done())
                        need(dve, exped, (u - 4).done())
                        src = K.S[u.slot % 2][:].rearrange("p (n k) -> p n k", k=wide)
                        dve.tensor_reduce(nmax[u.slot % 4][:], src[:, :, 0:keys], AX.X, ALU.max, negate=True).then_inc(maxed, 1)
                    if j == 0:
                        n = i + (-1 - behind)
                        if n.live:
                            need(dve, lnroot, n.done())
                            need(dve, stored[n.slot], (n - 4).landed())
                            dve.tensor_scalar(xo[n.slot][:], y[n.slot % 2][:], mv[n.slot % 2][:, 0:1], rs[n.slot % 2][:, 0:1],
                                              ALU.subtract, ALU.mult).then_inc(normed, 1)
                    v = u - 2
                    if v.live and v.slot % units == units - 1:
                        k = item(v)
                        need(dve, exped, v.done())
                        dve.reciprocal(inv[k.slot % 2][:], tot[k.slot][:]).then_inc(inverted, 1)
                        need(dve, inverted, k.done())
                        need(dve, inv_ps, (k - 2).done())
                        dve.tensor_copy(invx[k.slot % 2][:].rearrange("p (h d) -> p h d", h=NH),
                                        inv[k.slot % 2][:].rearrange("p (h a) -> p h a", a=1).to_broadcast([P, NH, HD])
                                        ).then_inc(spread, 1)
                pipeline(dve, step, uring, ucount, *span)

            @block.gpsimd
            def _(pool):
                def step(u):
                    j, i = u.slot % units, item(u)
                    b, n = i + 1, i + (-1 - behind)
                    if j == 0 and b.live:
                        need(pool, proj_sb, b.done())
                        need(pool, S_ps, (b - 2).done(units))
                    if j == 0 and n.live:
                        need(pool, meaned, n.done())
                        need(pool, normed, (n - 2).done())
                        pool.tensor_tensor(ve[n.slot % 2][:], mv[n.slot % 2][:, 1:2], K.eps[:], ALU.add).then_inc(eased, 1)
                        need(pool, eased, n.done())
                        pool.tensor_tensor(rs[n.slot % 2][:], ve[n.slot % 2][:], K.half[:, 0:1], ALU.pow).then_inc(lnroot, 1)
                    if b.live:
                        for h in heads(j):
                            last = pool.tensor_scalar(Qx[b.slot % 2][:, h, :], qk[b.slot][:, 0:P], K.headmask[:, h:h + 1],
                                                      1.0, ALU.mult, ALU.mult)
                        last.then_inc(masked, 1)
                pipeline(pool, step, uring, ucount, *span)
        K.clear()


def experts(K, D, tag, x_dram, out_dram, nseq):
    nc = K.nc
    units, T = EXPERTS + 1, 2 * P
    ring, count = 2, nseq // 2
    uring, ucount = ring * units, count * units
    x_pairs = x_dram.rearrange("(i a) p d -> i p a d", a=2)
    out_pairs = out_dram.rearrange("(i a) p d -> i p a d", a=2)

    def item(u):
        return At(u.p, u.slot // units, ring, count)

    K.taken = 0
    with ExitStack() as ctx:
        def sb(name, shape, dtype=F32):
            return K.sb(tag + name, shape, dtype, ctx)

        def sem(name):
            return K.sem(tag + name, ctx)

        x = [sb(f"x{i}", [P, 2, P]) for i in range(2)]
        xT = [sb(f"xT{i}", [P, T]) for i in range(2)]
        th = [sb(f"th{i}", [P, 2 * T]) for i in range(2)]
        gh = sb("gh", [P, 2 * T])
        gu = [sb(f"gu{i}", [P, 2, T]) for i in range(2)]
        acc = [sb(f"acc{i}", [P, 2, P]) for i in range(2)]
        best = [sb(f"best{i}", [P, 2, EXPERTS]) for i in range(2)]
        at = [sb(f"at{i}", [P, 2, EXPERTS], U32) for i in range(2)]
        atf = [sb(f"atf{i}", [P, 2, 2]) for i in range(2)]
        gap = [sb(f"gap{i}", [P, 2]) for i in range(2)]
        ex = [sb(f"ex{i}", [P, 2]) for i in range(2)]
        den = [sb(f"den{i}", [P, 2]) for i in range(2)]
        prob = [sb(f"prob{i}", [P, 2, 2]) for i in range(2)]
        part = [sb(f"part{i}", [P, 2, EXPERTS]) for i in range(2)]
        we = [sb(f"we{i}", [P, 2, EXPERTS]) for i in range(2)]
        logits = [sb(f"logits{i}", [P, 2, EXPERTS]) for i in range(2)]
        stats = [sb(f"st{i}", [P, 2, 6]) for i in range(2)]
        mv = [sb(f"mv{i}", [P, 2, 2]) for i in range(2)]
        ve = [sb(f"ve{i}", [P, 2]) for i in range(2)]
        rs = [sb(f"rs{i}", [P, 2]) for i in range(2)]
        xo = [sb(f"xo{i}", [P, 2, P]) for i in range(2)]

        x_in = [sem(f"x_in{i}") for i in range(2)]
        stored = [sem(f"stored{i}") for i in range(2)]
        xT_ps, gate_ps, hu_ps, out_ps = sem("xT_ps"), sem("gate_ps"), sem("hu_ps"), sem("out_ps")
        xT_sb, tanhed, opened, gated, added = sem("xT_sb"), sem("tanhed"), sem("opened"), sem("gated"), sem("added")
        picked, exped, weights = sem("picked"), sem("exped"), sem("weights")
        counted, meaned, eased, lnroot, normed = sem("counted"), sem("meaned"), sem("eased"), sem("lnroot"), sem("normed")

        W = K.W
        span = (-units, uring, (count - 1) // ring * ring * units, ucount + units)

        with nc.Block() as block:
            @block.sync
            def _(sp):
                def step(c):
                    a, o = c + 2, c - 2
                    if o.live:
                        need(sp, normed, o.done(2))
                        sp.dma_start(out_pairs[o.n], xo[o.slot][:]).then_inc(stored[o.slot], 16)
                    if a.live:
                        need(sp, added, (a - 2).done(2 * units, 2))
                        sp.dma_start(x[a.slot][:], x_pairs[a.n]).then_inc(x_in[a.slot], 16)
                pipeline(sp, step, ring, count, -2, 2, (count - 2) // ring * ring, count + 2)
                for i in range(ring):
                    sp.wait_ge(stored[i], 16 * len(range(i, count, ring)))

            @block.tensor
            def _(pe):
                def step(u):
                    j, i, t = u.slot % units, item(u), u - 2
                    b = i + 1
                    if t.live:
                        need(pe, gated, t.done())
                        need(pe, added, (t - 2).done(2))
                        e = t.slot % units
                        for half in range(2):
                            for blk in range(2):
                                last = pe.matmul(W[t.slot % 2][:, half * P:(half + 1) * P],
                                                 gu[t.slot % 2][:, blk, half * P:(half + 1) * P], K.e3[:, e, blk, :],
                                                 start=(blk == 0), stop=(blk == 1))
                        last.then_inc(out_ps, 1)
                    if u.live:
                        need(pe, xT_sb, i.done())
                        need(pe, gated, (u - 2).done())
                        for w, at0 in ((K.e1, 0), (K.e2, 512)):
                            for blk in range(2):
                                last = pe.matmul(K.S[u.slot % 2][:, at0 + blk * T:at0 + (blk + 1) * T],
                                                 w[:, j, blk * P:(blk + 1) * P], xT[i.slot][:], start=True, stop=True)
                        last.then_inc(hu_ps, 1)
                    if b.live and j == 3:
                        need(pe, x_in[b.slot], b.landed())
                        need(pe, picked, (b - 1).done(3))
                        pe.transpose(W[2][:, 0:P], x[b.slot][:, 0, :], K.ident[:])
                        pe.transpose(W[2][:, P:T], x[b.slot][:, 1, :], K.ident[:]).then_inc(xT_ps, 1)
                    if b.live and j == 5:
                        need(pe, xT_sb, b.done())
                        for half in range(2):
                            last = pe.matmul(W[2][:, T + half * EXPERTS:T + (half + 1) * EXPERTS],
                                             xT[b.slot][:, half * P:(half + 1) * P], K.gate[:], start=True, stop=True)
                        last.then_inc(gate_ps, 1)
                pipeline(pe, step, uring, ucount, *span)

            @block.scalar
            def _(act):
                def step(u):
                    j, i = u.slot % units, item(u)
                    b = i + 1
                    if u.live:
                        need(act, hu_ps, u.done())
                        need(act, opened, (u - 2).done())
                        act.activation(th[u.slot % 2][:], K.S[u.slot % 2][:, 0:2 * T], ACT.Tanh, scale=0.5).then_inc(tanhed, 1)
                    if b.live and j == 7:
                        need(act, picked, b.done(3, 2))
                        need(act, weights, (b - 2).done(10))
                        act.activation(ex[b.slot][:], gap[b.slot][:], ACT.Exp).then_inc(exped, 1)
                pipeline(act, step, uring, ucount, *span)

            @block.vector
            def _(dve):
                def choose(b):
                    need(dve, gate_ps, b.done())
                    need(dve, weights, (b - 2).done(10))
                    need(dve, exped, (b - 2).done())
                    dve.tensor_copy(logits[b.slot][:], W[2][:, T:T + 2 * EXPERTS].rearrange("p (a e) -> p a e", a=2))
                    for half in range(2):
                        last = dve.max(best[b.slot][:, half, :], W[2][:, T + half * EXPERTS:T + (half + 1) * EXPERTS])
                    last.then_inc(picked, 1)
                    dve.wait_ge(picked, b.done(3, 1))
                    dve.tensor_tensor(gap[b.slot][:], best[b.slot][:, :, 1], best[b.slot][:, :, 0],
                                      ALU.subtract).then_inc(picked, 1)
                    for half in range(2):
                        last = dve.max_index(at[b.slot][:, half, :], best[b.slot][:, half, :],
                                             W[2][:, T + half * EXPERTS:T + (half + 1) * EXPERTS])
                    last.then_inc(picked, 1)

                def weigh(b):
                    s = b.slot
                    need(dve, exped, b.done())
                    need(dve, picked, b.done(3))
                    need(dve, added, (b - 2).done(2 * units))
                    dve.tensor_scalar(den[s][:], ex[s][:], 2.0, 2.0, ALU.mult, ALU.add).then_inc(weights, 1)
                    dve.tensor_copy(atf[s][:], at[s][:, :, 0:2]).then_inc(weights, 1)
                    dve.wait_ge(weights, b.done(10, 1))
                    dve.reciprocal(prob[s][:, :, 0], den[s][:]).then_inc(weights, 1)
                    dve.wait_ge(weights, b.done(10, 3))
                    dve.tensor_tensor(prob[s][:, :, 1], prob[s][:, :, 0], ex[s][:], ALU.mult).then_inc(weights, 1)
                    dve.wait_ge(weights, b.done(10, 4))
                    for half in range(2):
                        for n, dst in enumerate((part, we)):
                            dve.tensor_scalar(dst[s][:, half, :], K.iota[:], atf[s][:, half, n:n + 1], prob[s][:, half, n:n + 1],
                                              ALU.is_equal, ALU.mult).then_inc(weights, 1)
                    dve.wait_ge(weights, b.done(10, 8))
                    for half in range(2):
                        dve.tensor_tensor(we[s][:, half, :], we[s][:, half, :], part[s][:, half, :], ALU.add).then_inc(weights, 1)

                def step(u):
                    j, i = u.slot % units, item(u)
                    b, t, g = i + 1, u - 3, u - 1
                    k = i - 1
                    if k.live and j == 3:
                        need(dve, added, k.done(2 * units))
                        for half in range(2):
                            last = dve.bn_stats(stats[k.slot][:, half, :], acc[k.slot][:, half, :])
                        last.then_inc(counted, 1)
                        need(dve, counted, k.done())
                    if t.live:
                        m, e = item(t), t.slot % units
                        need(dve, out_ps, t.done())
                        need(dve, weights, m.done(10))
                        if e == 0:
                            need(dve, normed, (m - 2).done(2))
                            need(dve, x_in[m.slot], m.landed())
                        else:
                            need(dve, added, (t - 1).done(2))
                        for half in range(2):
                            dve.scalar_tensor_tensor(
                                out=acc[m.slot][:, half, :], in0=W[t.slot % 2][:, half * P:(half + 1) * P],
                                scalar=0.5 if e == EXPERTS else we[m.slot][:, half, e:e + 1],
                                in1=(x if e == 0 else acc)[m.slot][:, half, :], op0=ALU.mult, op1=ALU.add).then_inc(added, 1)
                    if g.live:
                        need(dve, tanhed, g.done())
                        need(dve, gated, (g - 1).done())
                        dve.scalar_tensor_tensor(out=gh[:], in0=th[g.slot % 2][:], scalar=1.0, in1=K.S[g.slot % 2][:, 0:2 * T],
                                                 op0=ALU.add, op1=ALU.mult).then_inc(opened, 1)
                        need(dve, opened, g.done())
                        need(dve, out_ps, (g - 2).done())
                        dve.tensor_tensor(gu[g.slot % 2][:].rearrange("p b t -> p (b t)"), gh[:],
                                          K.S[g.slot % 2][:, 2 * T:4 * T], ALU.mult).then_inc(gated, 1)
                    if k.live and j == 3:
                        if not t.live and not g.live:
                            need(dve, counted, k.done())
                        for half in range(2):
                            last = dve.bn_aggr(mv[k.slot][:, half, :], stats[k.slot][:, half, :])
                        last.then_inc(meaned, 1)
                    if b.live and j == 3:
                        need(dve, xT_ps, b.done())
                        need(dve, hu_ps, (b - 2).done(units))
                        dve.tensor_copy(xT[b.slot][:], W[2][:, 0:T]).then_inc(xT_sb, 1)
                    if k.live and j == 5:
                        need(dve, lnroot, k.done())
                        need(dve, stored[k.slot], (k - 2).landed())
                        for half in range(2):
                            dve.tensor_scalar(xo[k.slot][:, half, :], acc[k.slot][:, half, :], mv[k.slot][:, half, 0:1],
                                              rs[k.slot][:, half:half + 1], ALU.subtract, ALU.mult).then_inc(normed, 1)
                    if b.live and j == 6:
                        choose(b)
                    if b.live and j == 8:
                        weigh(b)
                pipeline(dve, step, uring, ucount, *span)

            @block.gpsimd
            def _(pool):
                def step(k):
                    if k.live:
                        need(pool, meaned, k.done())
                        need(pool, normed, (k - 2).done(2))
                        pool.tensor_tensor(ve[k.slot][:], mv[k.slot][:, :, 1], K.eps[:].to_broadcast([P, 2]),
                                           ALU.add).then_inc(eased, 1)
                        need(pool, eased, k.done())
                        pool.tensor_tensor(rs[k.slot][:], ve[k.slot][:], K.half[:], ALU.pow).then_inc(lnroot, 1)
                pipeline(pool, step, ring, count, 0, 2, count // ring * ring, count)
        K.clear()


def ternary(K, D, tag, x_dram, out_dram, nseq):
    nc = K.nc
    ring = 4
    K.taken = 0
    with ExitStack() as ctx:
        def sb(name, shape, dtype=F32):
            return K.sb(tag + name, shape, dtype, ctx)

        def sem(name):
            return K.sem(tag + name, ctx)

        x = [sb(f"x{i}", [P, P]) for i in range(ring)]
        res = [sb(f"res{i}", [P, P]) for i in range(ring)]
        big = [sb(f"big{i}", [P, 4]) for i in range(ring)]
        zs = [sb(f"zs{i}", [P, 6]) for i in range(ring)]
        xr = [sb(f"xr{i}", [P, P]) for i in range(2)]
        xqT = [sb(f"xqT{i}", [P, P], BF16) for i in range(2)]
        th = [sb(f"th{i}", [P, INNER]) for i in range(2)]
        gh = sb("gh", [P, INNER])
        z = sb("z", [P, INNER])
        zr = [sb(f"zr{i}", [P, INNER]) for i in range(2)]
        zqT = [sb(f"zqT{i}", [P, INNER], BF16) for i in range(2)]
        y = [sb(f"y{i}", [P, P]) for i in range(2)]
        stats = [sb(f"st{i}", [P, 6]) for i in range(2)]
        mv = [sb(f"mv{i}", [P, 2]) for i in range(2)]
        ve = [sb(f"ve{i}", [P, 1]) for i in range(2)]
        rs = [sb(f"rs{i}", [P, 1]) for i in range(2)]
        xo = [sb(f"xo{i}", [P, P]) for i in range(ring)]

        x_in = [sem(f"x_in{i}") for i in range(ring)]
        res_in = [sem(f"res_in{i}") for i in range(ring)]
        stored = [sem(f"stored{i}") for i in range(ring)]
        xqT_ps, gu_ps, zqT_ps, out_ps = sem("xqT_ps"), sem("gu_ps"), sem("zqT_ps"), sem("out_ps")
        xqT_sb, zqT_sb, tanhed = sem("xqT_sb"), sem("zqT_sb"), sem("tanhed")
        xround, zround = sem("xround"), sem("zround")
        summed, counted, meaned, normed = sem("summed"), sem("counted"), sem("meaned"), sem("normed")
        eased, lnroot = sem("eased"), sem("lnroot")
        XR, ZR = 5, 9
        W = K.W
        span = (-4, 4, (nseq - 4) // ring * ring, nseq + 4)

        with nc.Block() as block:
            @block.sync
            def _(sp):
                def step(c):
                    a, o = c + 4, c - 4
                    if a.live:
                        need(sp, xround, (a - 4).done(XR))
                        sp.dma_start(x[a.slot][:], x_dram[a.n]).then_inc(x_in[a.slot], 16)
                    if c.live:
                        need(sp, summed, (c - 4).done())
                        sp.dma_start(res[c.slot][:], x_dram[c.n]).then_inc(res_in[c.slot], 16)
                    if o.live:
                        need(sp, normed, o.done())
                        sp.dma_start(out_dram[o.n], xo[o.slot][:]).then_inc(stored[o.slot], 16)
                pipeline(sp, step, ring, nseq, *span)
                for i in range(ring):
                    sp.wait_ge(stored[i], 16 * len(range(i, nseq, ring)))

            @block.tensor
            def _(pe):
                def step(c):
                    a, g, t, o = c + 2, c + 1, c - 1, c - 2
                    if t.live:
                        need(pe, zround, t.done(ZR))
                        need(pe, zqT_sb, (t - 1).done())
                        for n in range(4):
                            last = pe.transpose(W[1][:, n * P:(n + 1) * P], zr[t.slot % 2][:, n * P:(n + 1) * P], K.ident[:])
                        last.then_inc(zqT_ps, 1)
                    if g.live:
                        need(pe, xqT_sb, g.done())
                        need(pe, zround, (g - 2).done(ZR))
                        pe.matmul(K.S[g.slot % 2][:, 0:INNER], xqT[g.slot % 2][:], K.tg[:], start=True, stop=True)
                        pe.matmul(K.S[g.slot % 2][:, INNER:], xqT[g.slot % 2][:], K.tu[:], start=True, stop=True).then_inc(gu_ps, 1)
                    if a.live:
                        need(pe, xround, a.done(XR))
                        need(pe, xqT_sb, (a - 1).done())
                        pe.transpose(W[0][:, 0:P], xr[a.slot % 2][:], K.ident[:]).then_inc(xqT_ps, 1)
                    if o.live:
                        need(pe, zqT_sb, o.done())
                        need(pe, summed, (o - 1).done())
                        for n in range(4):
                            last = pe.matmul(W[2][:, 0:P], zqT[o.slot % 2][:, n * P:(n + 1) * P], K.td[:, n, :],
                                             start=(n == 0), stop=(n == 3))
                        last.then_inc(out_ps, 1)
                pipeline(pe, step, ring, nseq, *span)

            @block.scalar
            def _(act):
                def step(c):
                    a, g, t = c + 2, c + 1, c - 1
                    if t.live:
                        need(act, zqT_ps, t.done())
                        need(act, out_ps, (t - 2).done())
                        act.activation(zqT[t.slot % 2][:], W[1][:], ACT.Identity, bias=K.unround[:]).then_inc(zqT_sb, 1)
                    if g.live:
                        need(act, gu_ps, g.done())
                        need(act, zround, (g - 2).done(ZR))
                        act.activation(th[g.slot % 2][:], K.S[g.slot % 2][:, 0:INNER], ACT.Tanh,
                                       scale=big[g.slot][:, 3:4]).then_inc(tanhed, 1)
                    if a.live:
                        need(act, xqT_ps, a.done())
                        need(act, gu_ps, (a - 2).done())
                        act.activation(xqT[a.slot % 2][:], W[0][:, 0:P], ACT.Identity, bias=K.unround[:]).then_inc(xqT_sb, 1)
                pipeline(act, step, ring, nseq, *span)

            @block.vector
            def _(dve):
                def round_both(a, c):
                    b, s, g, S = big[a.slot], zs[c.slot], big[c.slot], K.S[c.slot % 2]
                    if c.live:
                        need(dve, tanhed, c.done())
                        need(dve, summed, (c - 4).done())
                        dve.scalar_tensor_tensor(out=gh[:], in0=th[c.slot % 2][:], scalar=1.0, in1=S[:, 0:INNER],
                                                 op0=ALU.add, op1=ALU.mult).then_inc(zround, 1)
                        dve.tensor_scalar(s[:, 0:1], g[:, 1:2], K.tmean[:, 1:2], g[:, 3:4], ALU.mult, ALU.mult).then_inc(zround, 1)
                    if a.live:
                        need(dve, x_in[a.slot], a.landed())
                        need(dve, zround, (a - 4).done(ZR))
                        dve.tensor_reduce(b[:, 0:1], x[a.slot][:], AX.X, ALU.max, apply_absolute_value=True).then_inc(xround, 1)
                    if c.live:
                        need(dve, zround, c.done(ZR, 1))
                        dve.tensor_tensor(z[:], gh[:], S[:, INNER:], ALU.mult).then_inc(zround, 1)
                    if a.live:
                        need(dve, xround, a.done(XR, 1))
                        dve.tensor_scalar(b[:, 1:2], b[:, 0:1], 1e-5, 1.0 / 127, ALU.max, ALU.mult).then_inc(xround, 1)
                    if c.live:
                        need(dve, zround, c.done(ZR, 3))
                        dve.tensor_reduce(s[:, 1:2], z[:], AX.X, ALU.max, apply_absolute_value=True).then_inc(zround, 1)
                    if a.live:
                        need(dve, xround, a.done(XR, 2))
                        dve.reciprocal(b[:, 2:3], b[:, 1:2]).then_inc(xround, 1)
                    if c.live:
                        need(dve, zround, c.done(ZR, 4))
                        dve.tensor_scalar(s[:, 2:3], s[:, 1:2], s[:, 0:1], 1e-5, ALU.mult, ALU.max).then_inc(zround, 1)
                    if a.live:
                        dve.tensor_scalar(b[:, 3:4], b[:, 1:2], K.tstep[:, 0:1], None, ALU.mult).then_inc(xround, 1)
                    if c.live:
                        need(dve, zround, c.done(ZR, 5))
                        dve.reciprocal(s[:, 3:4], s[:, 2:3]).then_inc(zround, 1)
                    if a.live:
                        need(dve, xround, a.done(XR, 3))
                        need(dve, xqT_ps, (a - 2).done())
                        dve.tensor_scalar(xr[a.slot % 2][:], x[a.slot][:], b[:, 2:3], ROUND, ALU.mult, ALU.add).then_inc(xround, 1)
                    if c.live:
                        need(dve, zround, c.done(ZR, 6))
                        dve.tensor_scalar(s[:, 4:5], s[:, 3:4], s[:, 0:1], 127.0, ALU.mult, ALU.mult).then_inc(zround, 1)
                        dve.tensor_scalar(s[:, 5:6], s[:, 2:3], K.tstep[:, 2:3], None, ALU.mult).then_inc(zround, 1)
                        need(dve, zround, c.done(ZR, 7))
                        need(dve, zqT_ps, (c - 2).done())
                        dve.tensor_scalar(zr[c.slot % 2][:], z[:], s[:, 4:5], ROUND, ALU.mult, ALU.add).then_inc(zround, 1)

                def step(c):
                    a, o, n = c + 3, c - 2, c - 3
                    round_both(a, c)
                    if o.live:
                        need(dve, out_ps, o.done())
                        need(dve, res_in[o.slot], o.landed())
                        need(dve, normed, (o - 2).done())
                        dve.scalar_tensor_tensor(out=y[o.slot % 2][:], in0=W[2][:, 0:P], scalar=zs[o.slot][:, 5:6],
                                                 in1=res[o.slot][:], op0=ALU.mult, op1=ALU.add).then_inc(summed, 1)
                        need(dve, summed, o.done())
                        dve.bn_stats(stats[o.slot % 2][:], y[o.slot % 2][:]).then_inc(counted, 1)
                        need(dve, counted, o.done())
                    if n.live:
                        need(dve, lnroot, n.done())
                        need(dve, stored[n.slot], (n - 4).landed())
                        dve.tensor_scalar(xo[n.slot][:], y[n.slot % 2][:], mv[n.slot % 2][:, 0:1], rs[n.slot % 2][:, 0:1],
                                          ALU.subtract, ALU.mult).then_inc(normed, 1)
                    if o.live:
                        dve.bn_aggr(mv[o.slot % 2][:], stats[o.slot % 2][:]).then_inc(meaned, 1)
                pipeline(dve, step, ring, nseq, *span)

            @block.gpsimd
            def _(pool):
                def step(n):
                    if n.live:
                        need(pool, meaned, n.done())
                        need(pool, normed, (n - 2).done())
                        pool.tensor_tensor(ve[n.slot % 2][:], mv[n.slot % 2][:, 1:2], K.eps[:], ALU.add).then_inc(eased, 1)
                        need(pool, eased, n.done())
                        pool.tensor_tensor(rs[n.slot % 2][:], ve[n.slot % 2][:], K.half[:, 0:1], ALU.pow).then_inc(lnroot, 1)
                pipeline(pool, step, ring, nseq, 0, 4, nseq // ring * ring, nseq)
        K.clear()


def constants():
    f = np.float32
    q, k = np.arange(P)[:, None], np.arange(P)[None, :]
    rel = k - q
    slopes = np.array([2.0 ** -h for h in range(WH)], f)
    alibi = np.where((rel > 0) | (rel < -16), f(-1e9), slopes[:, None, None] * rel.astype(f)).astype(f)
    inv_freq = (1.0 / 10000.0 ** (np.arange(0, HD, 2, dtype=f) / f(HD))).astype(f)
    freqs = (np.arange(P, dtype=f)[:, None] * inv_freq[None, :]).astype(f)
    spin = [np.tile(fn(freqs).astype(f).T, (2 * NH, 1)) for fn in (np.cos, np.sin)]
    gain = f(HD ** -0.5)
    return {
        "c_ident": np.eye(P, dtype=f),
        "c_alibi": np.ascontiguousarray(alibi.transpose(1, 0, 2).reshape(P, WH * P)),
        "c_iota": np.tile(np.arange(EXPERTS, dtype=f), (P, 1)),
        "c_causal": np.where(rel > 0, f(-255 * 2.0 ** 120), f(0)).astype(f),
        "c_headmask": (np.arange(P)[:, None] // HD == np.arange(NH)[None, :]).astype(f),
        "c_rope": np.ascontiguousarray(np.concatenate([spin[0] * gain, spin[0], spin[1] * gain, spin[1]], 1)),
    }


def build(nc, D, out, nseq):
    with ExitStack() as ctx:
        K = Core(nc, ctx)
        allocate(K)
        set_up(K, D)
        mid = [nc.dram_tensor(f"between{i}", [nseq, P, P], F32, kind="Internal").ap() for i in range(5)]
        attend_wide(K, D, "self0_", D["x"], mid[0], nseq, windowed=True)
        attend_narrow(K, D, "cross0_", mid[0], mid[1], nseq, cross=True)
        experts(K, D, "experts_", mid[1], mid[2], nseq)
        attend_narrow(K, D, "self1_", mid[2], mid[3], nseq, cross=False)
        attend_wide(K, D, "cross1_", mid[3], mid[4], nseq, windowed=False)
        ternary(K, D, "ternary_", mid[4], out, nseq)


def kernel(**inputs):
    import concourse.bacc as bacc
    from concourse.bass_utils import run_bass_kernel_spmd

    arrays = {name: np.ascontiguousarray(a) for name, a in inputs.items()}
    arrays.update(constants())
    nc = bacc.Bacc("TRN2", target_bir_lowering=False, num_devices=1)
    D = {name: nc.dram_tensor(f"in_{name}", a.shape, mybir.dt.from_np(a.dtype), kind="ExternalInput").ap()
         for name, a in arrays.items()}
    nseq = arrays["x"].shape[0]
    out = nc.dram_tensor("out", [nseq, P, P], F32, kind="ExternalOutput").ap()
    build(nc, D, out, nseq)
    r = run_bass_kernel_spmd(nc, [{f"in_{name}": a for name, a in arrays.items()}], core_ids=[0])
    return r.results[0]["out"]
```

```python
from contextlib import ExitStack

import numpy as np
import concourse.bass as bass
from concourse import mybir

F32 = mybir.dt.float32
BF16 = mybir.dt.bfloat16
U32 = mybir.dt.uint32
ALU = mybir.AluOpType
ACT = mybir.ActivationFunctionType
AX = mybir.AxisListType

P = 128
CTX = 120
WH = 8
NH = 16
HD = P // NH
EXPERTS = 8
HID = 256
INNER = 512
LN_EPS = 1e-5
RMS_EPS = 1e-6
ROUND = 1.5 * 2.0 ** 23


class At:

    def __init__(self, p, r, ring, count):
        self.p = p + r // ring if r // ring else p
        self.slot, self.ring, self.count = r % ring, ring, count

    def __add__(self, k):
        return At(self.p, self.slot + k, self.ring, self.count)

    def __sub__(self, k):
        return self + (-k)

    @property
    def n(self):
        return self.p * self.ring + self.slot if self.slot else self.p * self.ring

    @property
    def live(self):
        return not isinstance(self.p, int) or 0 <= self.n < self.count

    def done(self, per=1, part=None):
        return self.p * (self.ring * per) + (self.slot * per + (per if part is None else part))

    def landed(self):
        return self.p * 16 + 16


def need(eng, sem, value):
    if not isinstance(value, int) or value > 0:
        eng.wait_ge(sem, value)


def pipeline(eng, step, ring, count, first, lo, hi, last):
    for i in range(first, lo):
        step(At(i // ring, i % ring, ring, count))
    with eng.Fori(lo // ring, hi // ring) as p:
        for r in range(ring):
            step(At(p, r, ring, count))
    for i in range(hi, last):
        step(At(i // ring, i % ring, ring, count))


class Core:

    def __init__(self, nc, ctx):
        self.nc, self.ctx, self.taken, self.signals, self.stale = nc, ctx, 0, [], []
        self.holder, self.stale_holder = ExitStack(), ExitStack()
        self.small = self.sb("small", [P, 512])

    def sb(self, name, shape, dtype=F32, ctx=None):
        count = int(np.prod(shape[1:]))
        if ctx is None or count >= 64 or dtype == U32:
            return (ctx or self.ctx).enter_context(self.nc.sbuf_tensor(name, shape, dtype))
        part = self.small[:, self.taken:self.taken + count]
        self.taken += count
        return part if len(shape) == 2 else part.rearrange("p (a b) -> p a b", a=shape[1])

    def sem(self, name):
        self.signals.append(self.holder.enter_context(self.nc.semaphore(name)))
        return self.signals[-1]

    def clear(self, eng):
        for s in self.stale:
            eng.sem_clear(s)

    def passed(self, last=False):
        self.stale_holder.close()
        self.stale, self.stale_holder, self.signals, self.holder = self.signals, self.holder, [], ExitStack()
        if last:
            with self.nc.Block() as block:
                @block.gpsimd
                def _(pool):
                    self.clear(pool)
            self.stale_holder.close()


def allocate(K):
    K.S = [K.ctx.enter_context(K.nc.psum_tensor(f"psS{i}", [P, 1024], F32)) for i in range(2)]
    K.W = [K.ctx.enter_context(K.nc.psum_tensor(f"psW{i}", [P, 512], F32)) for i in range(4)]
    K.pr = [K.sb(f"pr{i}", [P, 1024]) for i in range(4)]
    K.ident = K.sb("ident", [P, P])
    K.identb = K.sb("identb", [P, P], BF16)
    K.alibi = K.sb("alibi", [P, WH * P])
    K.causal = K.sb("causal", [P, 4 * P], BF16)
    K.headmask = K.sb("headmask", [P, NH])
    K.rope = K.sb("rope", [P, 4 * P])
    K.unround = K.sb("unround", [P, 1])
    K.experts_in = K.ctx.enter_context(K.nc.semaphore("experts_in"))
    K.half = K.sb("half", [P, 2])
    K.eps = K.sb("eps", [P, 1])
    K.Mself = K.sb("Mself", [P, WH * P])
    K.Nself = K.sb("Nself", [P, WH * P])
    K.Gram = K.sb("Gram", [P, 2 * P])
    K.Mcross = K.sb("Mcross", [P, WH * P])
    K.Ncross = K.sb("Ncross", [P, WH * P])
    K.xw = K.sb("xw", [P, 4, P])
    K.xb = K.sb("xb", [P, 2])
    K.rowb = K.sb("rowb", [P, 3, P])
    K.rw = K.sb("rw", [P, 6, P])
    K.gate = K.sb("gate", [P, EXPERTS])
    K.e1 = K.sb("e1", [P, EXPERTS + 1, HID])
    K.e2 = K.sb("e2", [P, EXPERTS + 1, HID])
    K.e3 = K.sb("e3", [P, EXPERTS + 1, 2, P])
    K.tg = K.sb("tg", [P, INNER], BF16)
    K.tu = K.sb("tu", [P, INNER], BF16)
    K.td = K.sb("td", [P, 4, P], BF16)
    K.tmean = K.sb("tmean", [P, 3])
    K.tstep = K.sb("tstep", [P, 3])
    K.iota = K.sb("iota", [P, EXPERTS])


def set_up(K, D):
    nc = K.nc
    with ExitStack() as ctx:
        stage = K.sb("stage", [P, 3, WH * P], F32, ctx)
        stage2 = K.sb("stage2", [P, 3, 512], F32, ctx)
        wo = K.sb("wo", [P, WH, P], F32, ctx)
        wo2 = K.sb("wo2", [P, 4, P], F32, ctx)
        qkw = K.sb("qkw", [P, 2, WH], F32, ctx)
        qk = K.sb("qk", [P, WH], F32, ctx)
        wT = K.sb("wT", [P, 3, WH * P], F32, ctx)
        wTs = K.sb("wTs", [P, WH * P], F32, ctx)
        wT2 = K.sb("wT2", [P, 3, 512], F32, ctx)
        tern = K.sb("tern", [P, 3, 4, P], F32, ctx)
        ternq = K.sb("ternq", [P, 3, 4, P], F32, ctx)
        tabs = K.sb("tabs", [P, 3], F32, ctx)
        tsc = K.sb("tsc", [P, 3], F32, ctx)
        ones = K.sb("ones", [P, P], F32, ctx)
        first_in, w_in = K.sem("first_in"), K.sem("w_in")
        causal = K.sb("causal_in", [P, P], F32, ctx)
        made = K.sem("made")
        halved = K.sem("halved")
        pe_done = K.sem("pe_done")
        taken = K.sem("taken")
        banks = [K.S[0][:, 0:512], K.S[0][:, 512:1024], K.S[1][:, 0:512], K.S[1][:, 512:1024]] + [w[:] for w in K.W]

        first_loads = [
            (K.ident[:], D["c_ident"]),
            (stage[:, 0, :], D["L0_attn_wq"]), (stage[:, 1, :], D["L0_attn_wk"]), (stage[:, 2, :], D["L0_attn_wv"]),
            (wo[:], D["L0_attn_wo"].rearrange("(h e) n -> e h n", e=P)),
            (qkw[:, 0, :], D["L0_attn_q_norm_w"].rearrange("(h e) -> e h", e=P)),
            (qkw[:, 1, :], D["L0_attn_k_norm_w"].rearrange("(h e) -> e h", e=P)),
        ]
        loads = [
            (stage2[:, 0, :], D["L1_xattn_Wq"]), (stage2[:, 1, :], D["L1_xattn_Wk"]), (stage2[:, 2, :], D["L1_xattn_Wv"]),
            (wo2[:], D["L1_xattn_Wo"].rearrange("(b e) n -> e b n", e=P)),
            (tern[:, 0, :, :], D["L1_ffn_w_gate"].rearrange("(b o) i -> o b i", b=4)),
            (tern[:, 1, :, :], D["L1_ffn_w_up"].rearrange("(b o) i -> o b i", b=4)),
            (tern[:, 2, :, :], D["L1_ffn_w_down"].rearrange("o (b i) -> o b i", b=4)),
            (K.rw[:, 0:3, :], D["L1_attn_w_qkv"].rearrange("d (t n) -> d t n", t=3)),
            (K.rw[:, 5, :], D["L1_attn_w_out"]),
            (causal[:], D["c_causal"]), (K.alibi[:], D["c_alibi"]),
            (K.headmask[:], D["c_headmask"]), (K.rope[:], D["c_rope"]), (K.iota[:], D["c_iota"]),
            (K.xw[:, 0, :], D["L0_xattn_Wq"]), (K.xw[:, 1, :], D["L0_xattn_Wk"]),
            (K.xw[:, 2, :], D["L0_xattn_Wv"]), (K.xw[:, 3, :], D["L0_xattn_Wp"]),
            (K.xb[:, 0:1], D["L0_xattn_bq"].rearrange("(d a) -> d a", a=1)),
            (K.xb[:, 1:2], D["L0_xattn_bk"].rearrange("(d a) -> d a", a=1)),
            (K.rowb[:, 0, :], D["L0_xattn_bv"].rearrange("(a d) -> a d", a=1).to_broadcast([P, P])),
            (K.rowb[:, 1, :], D["L0_xattn_bp"].rearrange("(a d) -> a d", a=1).to_broadcast([P, P])),
            (K.rowb[:, 2, :], D["L1_xattn_bo"].rearrange("(a d) -> a d", a=1).to_broadcast([P, P])),
        ]
        expert_loads = [
            (K.gate[:], D["L0_ffn_gate_w"]),
            (K.e1[:, 0:EXPERTS, :], D["L0_ffn_ew1"].rearrange("e d f -> d e f")), (K.e1[:, EXPERTS, :], D["L0_ffn_sw1"]),
            (K.e2[:, 0:EXPERTS, :], D["L0_ffn_ew2"].rearrange("e d f -> d e f")), (K.e2[:, EXPERTS, :], D["L0_ffn_sw2"]),
            (K.e3[:, 0:EXPERTS, :, :], D["L0_ffn_ew3"].rearrange("e (b f) n -> f e b n", b=2)),
            (K.e3[:, EXPERTS, :, :], D["L0_ffn_sw3"].rearrange("(b f) n -> f b n", b=2)),
        ]
        FIRST, LOADED = 16 * len(first_loads), 16 * len(loads)
        K.EXPERTS_IN = 16 * len(expert_loads)

        cols = lambda j: slice(j * P, (j + 1) * P)
        turn = lambda srcs, dst: ([(cols(j), src, None, True, True) for j, src in enumerate(srcs)], dst)
        turns = [turn([stage[:, t, cols(4 * g + j)] for j in range(4)], wT[:, t, 512 * g:512 * g + 512])
                 for t in range(3) for g in range(2)]
        cross_turns = [turn([stage2[:, t, cols(j)] for j in range(4)], wT2[:, t, :]) for t in range(3)]
        ternary_turns = [turn([ternq[:, t, j, :] for j in range(4)], dst)
                         for t, dst in ((0, K.tg[:]), (1, K.tu[:]), (2, K.td[:].rearrange("p b n -> p (b n)")))]
        products, cross_products = [], []
        for g in range(2):
            h = [4 * g + j for j in range(4)]
            products.append(([(cols(j), wTs[:, cols(h[j])], wT[:, 1, cols(h[j])], True, True) for j in range(4)],
                             K.Mself[:, 512 * g:512 * g + 512]))
            products.append(([(cols(j), wT[:, 2, cols(h[j])], wo[:, h[j], :], True, True) for j in range(4)],
                             K.Nself[:, 512 * g:512 * g + 512]))
            row = slice(64 * g, 64 * g + 64)
            wide = lambda t: t[:].rearrange("p (j a n) -> p j a n", a=2, n=P)[:, :, g, :]
            cross_products.append(([(cols(j), wT2[row, 0, cols(j)], wT2[row, 1, cols(j)], True, True) for j in range(4)],
                                   wide(K.Mcross)))
            cross_products.append(([(cols(j), wT2[row, 2, cols(j)], wo2[row, j, :], True, True) for j in range(4)],
                                   wide(K.Ncross)))
        products.append(([(cols(t), wT[:, t, cols(h)], wT[:, t, cols(h)], h == 0, h == WH - 1)
                          for t in range(2) for h in range(WH)], K.Gram[:]))
        means = [([(slice(0, 3), ones[:], tabs[:], True, True)], None)]
        MEANS = len(turns + products + cross_turns)
        jobs = turns + products + cross_turns + means + cross_products + ternary_turns

        with nc.Block() as block:
            @block.sync
            def _(sp):
                for sem, some in ((first_in, first_loads), (w_in, loads), (K.experts_in, expert_loads)):
                    for dst, src in some:
                        sp.dma_start(dst, src, allow_slow_non_contiguous=True).then_inc(sem, 16)

            @block.gpsimd
            def _(pool):
                pool.memset(K.half[:], -0.5).then_inc(halved, 1)
                pool.memset(K.eps[:], LN_EPS).then_inc(halved, 1)
                pool.memset(K.unround[:], -ROUND).then_inc(halved, 1)
                pool.wait_ge(halved, 3)

            @block.vector
            def _(dve):
                dve.memset(ones[:], 1.0).then_inc(made, 1)
                dve.wait_ge(first_in, FIRST)
                dve.tensor_copy(K.identb[:], K.ident[:]).then_inc(made, 1)
                dve.tensor_tensor(qk[:], qkw[:, 0, :], qkw[:, 1, :], ALU.mult).then_inc(made, 1)
                dve.wait_ge(made, 3)
                dve.wait_ge(taken, 2)
                for h in range(WH):
                    dve.tensor_scalar(wTs[:, h * P:(h + 1) * P], wT[:, 0, h * P:(h + 1) * P], qk[:, h:h + 1], None,
                                      ALU.mult).then_inc(made, 1)
                dve.wait_ge(w_in, LOADED)
                for t in range(3):
                    dve.tensor_reduce(tabs[:, t:t + 1], tern[:, t, :, :].rearrange("p b i -> p (b i)"), AX.X,
                                      ALU.add, apply_absolute_value=True).then_inc(made, 1)
                for t in range(2):
                    w = K.rw[:, t, :].rearrange("p (h a d) -> p h a d", h=NH, a=2)
                    r = K.rw[:, 3 + t, :].rearrange("p (h a d) -> p h a d", h=NH, a=2)
                    dve.tensor_scalar(r[:, :, 0, :], w[:, :, 1, :], -1.0, None, ALU.mult).then_inc(made, 1)
                    dve.tensor_copy(r[:, :, 1, :], w[:, :, 0, :]).then_inc(made, 1)
                for h in range(4):
                    dve.tensor_copy(K.causal[:, h * P:(h + 1) * P], causal[:])
                dve.wait_ge(pe_done, MEANS + 1)
                dve.tensor_scalar(K.tmean[:], banks[MEANS % 8][:, 0:3], 1.0 / (INNER * P), 1e-5, ALU.mult,
                                  ALU.max).then_inc(made, 1)
                dve.wait_ge(made, 19)
                dve.reciprocal(tsc[:], K.tmean[:]).then_inc(made, 1)
                dve.wait_ge(made, 20)
                for t in range(3):
                    dve.tensor_scalar(ternq[:, t, :, :], tern[:, t, :, :], tsc[:, t:t + 1], ROUND, ALU.mult,
                                      ALU.add).then_inc(made, 1)
                dve.wait_ge(made, 23)
                for t in range(3):
                    dve.tensor_scalar(ternq[:, t, :, :], ternq[:, t, :, :], ROUND, 1.0, ALU.subtract,
                                      ALU.min).then_inc(made, 1)
                dve.wait_ge(made, 26)
                for t in range(3):
                    dve.tensor_scalar(ternq[:, t, :, :], ternq[:, t, :, :], -1.0, None, ALU.max).then_inc(made, 1)
                dve.tensor_scalar(K.tstep[:, 0:1], K.tmean[:, 0:1], 0.5, None, ALU.mult).then_inc(made, 1)
                dve.tensor_scalar(K.tstep[:, 2:3], K.tmean[:, 2:3], 1.0 / 127.0, None, ALU.mult).then_inc(made, 1)

            @block.tensor
            def _(pe):
                pe.wait_ge(first_in, FIRST)
                for n, (mms, _) in enumerate(jobs):
                    if n == len(turns):
                        pe.wait_ge(made, 11)
                        pe.wait_ge(taken, len(turns))
                    if n == len(turns + products):
                        pe.wait_ge(w_in, LOADED)
                    if n == MEANS:
                        pe.wait_ge(made, 14)
                    if n == MEANS + 1:
                        pe.wait_ge(taken, MEANS)
                    if n == len(jobs) - len(ternary_turns):
                        pe.wait_ge(made, 29)
                    if n >= 8:
                        pe.wait_ge(taken, n - 7)
                    for c, lhsT, rhs, start, stop in mms:
                        if rhs is None:
                            last = pe.transpose(banks[n % 8][:, c], lhsT, K.ident[:])
                        else:
                            last = pe.matmul(banks[n % 8][:, c], lhsT, rhs, start=start, stop=stop)
                    last.then_inc(pe_done, 1)

            @block.scalar
            def _(act):
                for n, (_, dst) in enumerate(jobs):
                    if n == MEANS:
                        act.wait_ge(made, 19)
                        act.drain().then_inc(taken, 1)
                        continue
                    act.wait_ge(pe_done, n + 1)
                    src = banks[n % 8]
                    src = src.rearrange("p (j n) -> p j n", n=P) if len(dst.shape) == 3 else src[:, 0:dst.shape[1]]
                    act.copy(dst, src).then_inc(taken, 1)
        K.passed()


def attend_wide(K, D, tag, x_dram, out_dram, nseq, windowed, last_pass=False):
    nc = K.nc
    ring = 4
    keys = P if windowed else CTX
    M, N = (K.Mself, K.Nself) if windowed else (K.Mcross, K.Ncross)
    early = 6 if windowed else 8
    last_gain = P ** -0.5 if windowed else 64 ** -0.5
    feed = not windowed
    scores = K.S if windowed else [K.S[0], K.S[0]]
    K.taken = 0
    with ExitStack() as ctx:
        def sb(name, shape, dtype=F32):
            return K.sb(tag + name, shape, dtype, ctx)

        def sem(name):
            return K.sem(tag + name)

        x = [sb(f"x{i}", [P, P]) for i in range(ring)]
        cx = [sb(f"cx{i}", [P, P]) for i in range(ring)]
        res = [sb(f"res{i}", [P, P]) for i in range(ring)]
        xT = [sb(f"xT{i}", [P, P]) for i in range(ring)]
        xs = [sb(f"xs{i}", [P, 2 * P]) for i in range(2)]
        sT = [sb(f"sT{i}", [P, 2 * P]) for i in range(ring)]
        junk = sb("junk", [P, P])
        ss = [sb(f"ss{i}", [P, 2]) for i in range(2)]
        rms = [sb(f"rms{i}", [P, 2]) for i in range(2)]
        xM = [sb(f"xM{i}", [P, WH * P]) for i in range(2)]
        U = [sb(f"U{i}", [P, WH * P]) for i in range(ring)]
        pr = K.pr
        nmax = [sb(f"nmax{i}", [P, WH]) for i in range(2)]
        tot = [sb(f"tot{i}", [P, WH]) for i in range(ring)]
        inv = [sb(f"inv{i}", [P, WH]) for i in range(ring)]
        pT = [sb(f"pT{i}", [P, WH * P]) for i in range(2)]
        y = [sb(f"y{i}", [P, P]) for i in range(2)]
        yb = sb("yb", [P, P])
        stats = [sb(f"st{i}", [P, 6]) for i in range(2)]
        mv = [sb(f"mv{i}", [P, 2]) for i in range(2)]
        ve = [sb(f"ve{i}", [P, 1]) for i in range(2)]
        rs = [sb(f"rs{i}", [P, 1]) for i in range(2)]
        xo = [sb(f"xo{i}", [P, P]) for i in range(ring)]
        if feed:
            big = [sb(f"big{i}", [P, 4]) for i in range(ring)]
            zs = [sb(f"zs{i}", [P, 6]) for i in range(ring)]
            xr = [sb(f"xr{i}", [P, P]) for i in range(2)]
            xqT = sb("xqT", [P, P], BF16)
            th = sb("th", [P, INNER])
            gh = sb("gh", [P, INNER])
            z = sb("z", [P, INNER])
            zr = sb("zr", [P, INNER])
            zqT = sb("zqT", [P, INNER], BF16)
            fy = [sb(f"fy{i}", [P, P]) for i in range(2)]
            fstats = [sb(f"fst{i}", [P, 6]) for i in range(2)]
            fmv = [sb(f"fmv{i}", [P, 2]) for i in range(2)]
            fve = [sb(f"fve{i}", [P, 1]) for i in range(2)]
            frs = [sb(f"frs{i}", [P, 1]) for i in range(2)]
            fxo = [sb(f"fxo{i}", [P, P]) for i in range(ring)]
            xqT_ps, gu_ps, zqT_ps, fout_ps = sem("xqT_ps"), sem("gu_ps"), sem("zqT_ps"), sem("fout_ps")
            xqT_sb, zqT_sb, tanhed = sem("xqT_sb"), sem("zqT_sb"), sem("tanhed")
            xround, zround = sem("xround"), sem("zround")
            fsummed, fcounted, fmeaned, fnormed = sem("fsummed"), sem("fcounted"), sem("fmeaned"), sem("fnormed")
            feased, flnroot = sem("feased"), sem("flnroot")
        XR, ZR = 5, 9

        x_in = [sem(f"x_in{i}") for i in range(ring)]
        cx_in = [sem(f"cx_in{i}") for i in range(ring)]
        res_in = [sem(f"res_in{i}") for i in range(ring)]
        stored = [sem(f"stored{i}") for i in range(ring)]
        xT_ps, sT_ps, gram_ps, xM_ps = sem("xT_ps"), sem("sT_ps"), sem("gram_ps"), sem("xM_ps")
        S_ps, U_ps, pT_ps, out_ps = sem("S_ps"), sem("U_ps"), sem("pT_ps"), sem("out_ps")
        xM_sb, U_sb, exped = sem("xM_sb"), sem("U_sb"), sem("exped")
        xT_sb, sT_sb, pT_sb, squared, scaled = sem("xT_sb"), sem("sT_sb"), sem("pT_sb"), sem("squared"), sem("scaled")
        biased, maxed, inverted, summed = sem("biased"), sem("maxed"), sem("inverted"), sem("summed")
        counted, meaned, normed = sem("counted"), sem("meaned"), sem("normed")
        joined = sem("joined")
        rooted, eased, lnroot, weighed = sem("rooted"), sem("eased"), sem("lnroot"), sem("weighed")

        W = K.W
        span = (-5, 12 if feed else 8, (nseq - 5) // ring * ring, nseq + (8 if feed else 5) + 1)

        with nc.Block() as block:
            @block.sync
            def _(sp):
                def step(c):
                    a = c + 5
                    if a.live:
                        need(sp, scaled if windowed else xT_ps, (a - 4).done(2 if windowed else 1))
                        sp.dma_start(x[a.slot][:], x_dram[a.n]).then_inc(x_in[a.slot], 16)
                        if not windowed:
                            sp.dma_start(cx[a.slot][0:CTX, :], D["ctx_1024"][a.n]).then_inc(cx_in[a.slot], 16)
                    if c.live:
                        need(sp, summed, (c - 4).done())
                        sp.dma_start(res[c.slot][:], x_dram[c.n]).then_inc(res_in[c.slot], 16)
                    o = c - (8 if feed else 5)
                    if o.live:
                        need(sp, fnormed if feed else normed, o.done())
                        sp.dma_start(out_dram[o.n], (fxo if feed else xo)[o.slot][:]).then_inc(stored[o.slot], 16)
                pipeline(sp, step, ring, nseq, *span)
                for i in range(ring):
                    sp.wait_ge(stored[i], 16 * len(range(i, nseq, ring)))

            @block.tensor
            def _(pe):
                def feed_out(o):
                    if feed and o.live:
                        need(pe, zqT_sb, o.done())
                        for n in range(4):
                            last = pe.matmul(K.S[1][:, INNER:INNER + P], zqT[:, n * P:(n + 1) * P], K.td[:, n, :],
                                             start=(n == 0), stop=(n == 3))
                        last.then_inc(fout_ps, 1)

                def feed_turn_x(f):
                    if feed and f.live:
                        need(pe, xround, f.done(XR))
                        need(pe, fsummed, (f - 1).done())
                        pe.transpose(K.S[1][:, INNER:INNER + P], xr[f.slot % 2][:], K.ident[:]).then_inc(xqT_ps, 1)

                def feed_gate_up(f):
                    if feed and f.live:
                        need(pe, xqT_sb, f.done())
                        pe.matmul(K.S[1][:, 0:INNER], xqT[:], K.tg[:], start=True, stop=True)
                        pe.matmul(K.S[1][:, INNER:], xqT[:], K.tu[:], start=True, stop=True).then_inc(gu_ps, 1)

                def feed_turn_z(f):
                    if feed and f.live:
                        need(pe, zround, f.done(ZR))
                        for n in range(4):
                            last = pe.transpose(K.S[1][:, n * P:(n + 1) * P], zr[:, n * P:(n + 1) * P], K.ident[:])
                        last.then_inc(zqT_ps, 1)

                def output(t, heads):
                    if t.live:
                        for h in heads:
                            last = pe.matmul(W[3][:, 0:P], pT[t.slot % 2][0:keys, h * P:(h + 1) * P],
                                             U[t.slot][0:keys, h * P:(h + 1) * P], start=(h == 0), stop=(h == WH - 1))
                            if h == WH - 1:
                                last.then_inc(out_ps, 1)

                def turn_inputs(b, m, g, a):
                    if b.live:
                        need(pe, U_sb, b.done(2))
                    elif m.live:
                        need(pe, xM_sb, m.done(2))
                    if g.live and windowed:
                        need(pe, scaled, g.done(2))
                        pe.transpose(W[2][:, P:2 * P], xs[g.slot % 2][:, 0:P], K.ident[:])
                        pe.transpose(W[2][:, 2 * P:3 * P], xs[g.slot % 2][:, P:2 * P], K.ident[:]).then_inc(sT_ps, 1)
                    if a.live:
                        if not b.live:
                            need(pe, xT_sb, (a - 1).done())
                        need(pe, x_in[a.slot], a.landed())
                        last = pe.transpose(W[2][:, 0:P], x[a.slot][:], K.ident[:])
                        if not windowed:
                            need(pe, cx_in[a.slot], a.landed())
                            last = pe.transpose(W[2][:, P:P + CTX], cx[a.slot][0:CTX, :], K.ident[0:CTX, 0:CTX])
                        last.then_inc(xT_ps, 1)

                def step(c):
                    t, m, g, b, a = c - 3, c + 1, c + 2, c, c + 3
                    if t.live:
                        need(pe, weighed, t.done(2))
                        if (c + 1).live and windowed:
                            need(pe, squared, (c + 1).done(2))
                        need(pe, pT_sb, (t - 1).done(2))
                        need(pe, U_sb, (c - 1).done(2) if (c - 1).live else 0)
                        for half in range(2):
                            for j in range(4):
                                h = 4 * half + j
                                last = pe.transpose(W[half][0:keys, j * P:(j + 1) * P],
                                                    pr[t.slot][:, h * P:h * P + keys], K.ident[:])
                            last.then_inc(pT_ps, 1)
                    if m.live:
                        if windowed:
                            need(pe, sT_sb, m.done())
                        need(pe, xT_sb, (c + 2).done() if (c + 2).live else m.done())
                    for half in range(2):
                        if half == 0:
                            feed_out(c - 6)
                        else:
                            feed_turn_x(c - 5)
                        if m.live:
                            if half == 1:
                                need(pe, summed, (t - 1).done())
                            for j in range(4):
                                h = 4 * half + j
                                last = pe.matmul(W[2 + half][:, j * P:(j + 1) * P], M[:, h * P:(h + 1) * P],
                                                 sT[m.slot][:, 0:P] if windowed else xT[m.slot][:],
                                                 start=True, stop=True)
                            last.then_inc(xM_ps, 1)
                    feed_gate_up(c - 5)
                    if g.live and windowed:
                        need(pe, xT_sb, g.done())
                        need(pe, pT_sb, t.done(2, 1))
                        pe.matmul(W[0][:, 0:2 * P], xT[g.slot][:], K.Gram[:], start=True, stop=True).then_inc(gram_ps, 1)
                    if b.live:
                        need(pe, xM_sb, b.done(2))
                        if windowed:
                            need(pe, biased, (b - 2).done())
                        else:
                            need(pe, exped, (b - 1).done(2))
                        for h in range(WH):
                            last = pe.matmul(scores[b.slot % 2][:, h * P:h * P + keys], xM[b.slot % 2][:, h * P:(h + 1) * P],
                                             sT[b.slot][:, P:P + keys], start=True, stop=True)
                        last.then_inc(S_ps, 1)
                    if b.live:
                        need(pe, pT_sb, t.done(2))
                        if m.live:
                            need(pe, xM_sb, m.done(2, 1))
                        for half in range(2):
                            pe.matmul(W[1 + half][0:keys, :], (xT[b.slot][:] if windowed else sT[b.slot][:, P:P + keys]),
                                      N[:, 512 * half:512 * half + 512], start=True, stop=True).then_inc(U_ps, 1)
                    if t.live:
                        need(pe, pT_sb, t.done(2))
                        need(pe, U_sb, t.done(2))
                        if m.live:
                            need(pe, xM_sb, m.done(2))
                        need(pe, summed, (t - 1).done())
                    output(t, range(0, early))
                    turn_inputs(b, m, g, a)
                    output(t, range(early, WH))
                    feed_turn_z(c - 5)
                pipeline(pe, step, ring, nseq, *span)

            @block.scalar
            def _(act):
                def copy_xM(m, halves):
                    for half in halves:
                        need(act, xM_ps, m.done(2, half + 1))
                        need(act, S_ps, (m - 2).done())
                        act.activation(xM[m.slot % 2][:, 512 * half:512 * half + 512], W[2 + half][:], ACT.Copy,
                                       scale=1.0 if windowed else last_gain).then_inc(xM_sb, 1)

                def exps(e, heads):
                    src = pr[e.slot] if windowed else K.S[0]
                    if heads[0] == 0:
                        need(act, inverted, (e - 4).done())
                        need(act, maxed, e.done())
                        need(act, pT_ps, (e - 4).done(2))
                    for h in heads:
                        last = act.activation(pr[e.slot][:, h * P:h * P + keys], src[:, h * P:h * P + keys], ACT.Exp,
                                              bias=nmax[e.slot % 2][:, h:h + 1], accum_out=tot[e.slot][:, h:h + 1])
                        if h % 4 == 3:
                            last.then_inc(exped, 1)

                def copy_U(b, half):
                    if half == 0:
                        need(act, out_ps, (b - 4).done())
                    need(act, U_ps, b.done(2, half + 1))
                    act.copy(U[b.slot][0:keys, 512 * half:512 * half + 512], W[1 + half][0:keys, :]).then_inc(U_sb, 1)

                def step(c):
                    m, e, b = c + 1, c - 1, c
                    if m.live:
                        copy_xM(m, range(2))
                    for h in range(WH):
                        if e.live:
                            exps(e, range(h, h + 1))
                        if b.live and h in (4, 6):
                            copy_U(b, (h - 4) // 2)

                def step_feed(c):
                    m, f, b = c + 1, c - 5, c
                    if m.live:
                        copy_xM(m, range(1))
                    if f.live:
                        need(act, xqT_ps, f.done())
                        need(act, gu_ps, (f - 1).done())
                        act.activation(xqT[:], K.S[1][:, INNER:INNER + P], ACT.Identity, bias=K.unround[:]).then_inc(xqT_sb, 1)
                    if m.live:
                        copy_xM(m, range(1, 2))
                    if f.live:
                        need(act, gu_ps, f.done())
                        need(act, zround, (f - 1).done(ZR))
                        act.activation(th[:], K.S[1][:, 0:INNER], ACT.Tanh, scale=big[f.slot][:, 3:4]).then_inc(tanhed, 1)
                    if b.live:
                        exps(b, range(0, 1))
                        copy_U(b, 0)
                        exps(b, range(1, 2))
                        copy_U(b, 1)
                        exps(b, range(2, 6))
                    if f.live:
                        need(act, zqT_ps, f.done())
                        need(act, fout_ps, (f - 1).done())
                        act.activation(zqT[:], K.S[1][:, 0:INNER], ACT.Identity, bias=K.unround[:]).then_inc(zqT_sb, 1)
                    if b.live:
                        exps(b, range(6, 8))
                pipeline(act, step_feed if feed else step, ring, nseq, *span)

            @block.vector
            def _(dve):
                def feed_sum(o):
                    need(dve, fout_ps, o.done())
                    need(dve, fnormed, (o - 2).done())
                    dve.scalar_tensor_tensor(out=fy[o.slot % 2][:], in0=K.S[1][:, INNER:INNER + P], scalar=zs[o.slot][:, 5:6],
                                             in1=xo[o.slot][:], op0=ALU.mult, op1=ALU.add).then_inc(fsummed, 1)
                    need(dve, fsummed, o.done())
                    dve.bn_stats(fstats[o.slot % 2][:], fy[o.slot % 2][:]).then_inc(fcounted, 1)

                def feed_round_x(a):
                    b = big[a.slot]
                    need(dve, normed, a.done())
                    need(dve, zround, (a - 4).done(ZR))
                    dve.tensor_reduce(b[:, 0:1], xo[a.slot][:], AX.X, ALU.max, apply_absolute_value=True).then_inc(xround, 1)
                    need(dve, xround, a.done(XR, 1))
                    dve.tensor_scalar(b[:, 1:2], b[:, 0:1], 1e-5, 1.0 / 127, ALU.max, ALU.mult).then_inc(xround, 1)
                    need(dve, xround, a.done(XR, 2))
                    dve.reciprocal(b[:, 2:3], b[:, 1:2]).then_inc(xround, 1)
                    dve.tensor_scalar(b[:, 3:4], b[:, 1:2], K.tstep[:, 0:1], None, ALU.mult).then_inc(xround, 1)
                    need(dve, xround, a.done(XR, 3))
                    need(dve, xqT_ps, (a - 2).done())
                    dve.tensor_scalar(xr[a.slot % 2][:], xo[a.slot][:], b[:, 2:3], ROUND, ALU.mult, ALU.add).then_inc(xround, 1)

                def feed_silu(c):
                    s, g = zs[c.slot], big[c.slot]
                    need(dve, tanhed, c.done())
                    need(dve, fsummed, (c - 4).done())
                    dve.scalar_tensor_tensor(out=gh[:], in0=th[:], scalar=1.0, in1=K.S[1][:, 0:INNER],
                                             op0=ALU.add, op1=ALU.mult).then_inc(zround, 1)
                    dve.tensor_scalar(s[:, 0:1], g[:, 1:2], K.tmean[:, 1:2], g[:, 3:4], ALU.mult, ALU.mult).then_inc(zround, 1)
                    need(dve, zround, c.done(ZR, 1))
                    dve.tensor_tensor(z[:], gh[:], K.S[1][:, INNER:], ALU.mult).then_inc(zround, 1)

                def feed_round_z(c):
                    s = zs[c.slot]
                    need(dve, zround, c.done(ZR, 3))
                    dve.tensor_reduce(s[:, 1:2], z[:], AX.X, ALU.max, apply_absolute_value=True).then_inc(zround, 1)
                    need(dve, zround, c.done(ZR, 4))
                    dve.tensor_scalar(s[:, 2:3], s[:, 1:2], s[:, 0:1], 1e-5, ALU.mult, ALU.max).then_inc(zround, 1)
                    need(dve, zround, c.done(ZR, 5))
                    dve.reciprocal(s[:, 3:4], s[:, 2:3]).then_inc(zround, 1)
                    dve.tensor_scalar(s[:, 5:6], s[:, 2:3], K.tstep[:, 2:3], None, ALU.mult).then_inc(zround, 1)
                    need(dve, zround, c.done(ZR, 6))
                    dve.tensor_scalar(s[:, 4:5], s[:, 3:4], s[:, 0:1], 127.0, ALU.mult, ALU.mult).then_inc(zround, 1)
                    need(dve, zround, c.done(ZR, 8))
                    need(dve, zqT_ps, (c - 1).done())
                    dve.tensor_scalar(zr[:], z[:], s[:, 4:5], ROUND, ALU.mult, ALU.add).then_inc(zround, 1)

                def sum_output(t):
                    if t.live:
                        dve.wait_ge(res_in[t.slot], t.landed())
                        need(dve, normed, (t - 2).done())
                        if not windowed:
                            dve.tensor_tensor(yb[:], res[t.slot][:], K.rowb[:, 2, :], ALU.add).then_inc(joined, 1)
                            dve.wait_ge(joined, t.done())
                        dve.wait_ge(out_ps, t.done())
                        dve.tensor_tensor(y[t.slot % 2][:], W[3][:, 0:P], (res[t.slot] if windowed else yb)[:],
                                          ALU.add).then_inc(summed, 1)
                        dve.wait_ge(summed, t.done())
                        dve.bn_stats(stats[t.slot % 2][:], y[t.slot % 2][:]).then_inc(counted, 1)

                def step(c):
                    t, n, g, b, e, a = c - 3, c - 4, c + 2, c, c - 1, c + 3
                    o, p = c - 6, c - 7
                    if t.live:
                        need(dve, out_ps, (t - 2).done())
                        for half in range(2):
                            need(dve, pT_ps, t.done(2, half + 1))
                            if half == 1 and n.live:
                                dve.wait_ge(counted, n.done())
                            dve.tensor_copy(pT[t.slot % 2][0:keys, 512 * half:512 * half + 512],
                                            W[half][0:keys, :]).then_inc(pT_sb, 1)
                    if n.live:
                        if not t.live:
                            dve.wait_ge(counted, n.done())
                        dve.bn_aggr(mv[n.slot % 2][:], stats[n.slot % 2][:]).then_inc(meaned, 1)
                    if feed and o.live:
                        feed_sum(o)
                    if n.live:
                        if feed and o.live:
                            need(dve, fcounted, o.done())
                        dve.wait_ge(lnroot, n.done())
                        if not feed:
                            need(dve, stored[n.slot], (n - 4).landed())
                        dve.tensor_scalar(xo[n.slot][:], y[n.slot % 2][:], mv[n.slot % 2][:, 0:1], rs[n.slot % 2][:, 0:1],
                                          ALU.subtract, ALU.mult).then_inc(normed, 1)
                    elif feed and o.live:
                        dve.wait_ge(fcounted, o.done())
                    if feed and o.live:
                        dve.bn_aggr(fmv[o.slot % 2][:], fstats[o.slot % 2][:]).then_inc(fmeaned, 1)
                    if feed and n.live:
                        feed_round_x(n)
                    if g.live and windowed:
                        dve.wait_ge(gram_ps, g.done())
                        need(dve, rooted, (g - 2).done())
                        for k in range(2):
                            if k == 1:
                                dve.wait_ge(squared, g.done(2, 1))
                            else:
                                need(dve, squared, (g - 1).done(2))
                            dve.tensor_tensor_reduce(out=junk[:], in0=W[0][:, k * P:(k + 1) * P], in1=x[g.slot][:],
                                                     scale=1.0 / (WH * P), scalar=RMS_EPS, op0=ALU.mult, op1=ALU.add,
                                                     accum_out=ss[g.slot % 2][:, k:k + 1]).then_inc(squared, 1)
                    if feed and e.live:
                        dve.wait_ge(exped, e.done(2))
                        need(dve, weighed, (e - 4).done(2))
                        dve.reciprocal(inv[e.slot][:], tot[e.slot][:]).then_inc(inverted, 1)
                    if feed and (c - 5).live:
                        feed_silu(c - 5)
                    if g.live and windowed:
                        dve.wait_ge(rooted, g.done())
                        need(dve, sT_ps, (g - 2).done())
                        dve.tensor_scalar(xs[g.slot % 2][:, 0:P], x[g.slot][:], rms[g.slot % 2][:, 0:1], last_gain,
                                          ALU.mult, ALU.mult).then_inc(scaled, 1)
                        dve.tensor_scalar(xs[g.slot % 2][:, P:2 * P], x[g.slot][:], rms[g.slot % 2][:, 1:2], None,
                                          ALU.mult).then_inc(scaled, 1)
                    if b.live:
                        dve.wait_ge(S_ps, b.done())
                        src = scores[b.slot % 2][:]
                        need(dve, exped, (b - 2).done(2))
                        if windowed:
                            need(dve, pT_ps, (b - 4).done(2))
                            dve.tensor_tensor(pr[b.slot][:], K.S[b.slot % 2][:], K.alibi[:], ALU.add).then_inc(biased, 1)
                            src = pr[b.slot][:]
                            dve.wait_ge(biased, b.done())
                        dve.tensor_reduce(nmax[b.slot % 2][:], src.rearrange("p (h k) -> p h k", h=WH)[:, :, 0:keys],
                                          AX.X, ALU.max, negate=True).then_inc(maxed, 1)
                    if windowed and e.live:
                        dve.wait_ge(exped, e.done(2))
                        need(dve, weighed, (e - 4).done(2))
                        dve.reciprocal(inv[e.slot][:], tot[e.slot][:]).then_inc(inverted, 1)
                    if feed and (c - 5).live:
                        feed_round_z(c - 5)
                    if feed and p.live:
                        need(dve, flnroot, p.done())
                        need(dve, stored[p.slot], (p - 4).landed())
                        dve.tensor_scalar(fxo[p.slot][:], fy[p.slot % 2][:], fmv[p.slot % 2][:, 0:1], frs[p.slot % 2][:, 0:1],
                                          ALU.subtract, ALU.mult).then_inc(fnormed, 1)
                    if feed:
                        sum_output(t)
                    if g.live and windowed:
                        dve.wait_ge(sT_ps, g.done())
                        if a.live:
                            dve.wait_ge(xT_ps, a.done())
                        need(dve, S_ps, (g - 4).done())
                        dve.tensor_copy(sT[g.slot][:], W[2][:, P:3 * P]).then_inc(sT_sb, 1)
                    if a.live:
                        dve.wait_ge(xT_ps, a.done())
                        need(dve, U_ps, (a - 4).done(2))
                        if not windowed:
                            need(dve, S_ps, (a - 4).done())
                            dve.tensor_copy(sT[a.slot][:, P:P + CTX], W[2][:, P:P + CTX])
                        dve.tensor_copy(xT[a.slot][:], W[2][:, 0:P]).then_inc(xT_sb, 1)
                    if windowed:
                        sum_output(t)
                pipeline(dve, step, ring, nseq, *span)

            @block.gpsimd
            def _(pool):
                K.clear(pool)

                def weigh(w, half):
                    for h in range(4 * half, 4 * half + 4):
                        last = pool.tensor_scalar(pr[w.slot][:, h * P:h * P + keys], pr[w.slot][:, h * P:h * P + keys],
                                                  inv[w.slot][:, h:h + 1], 1.0, ALU.mult, ALU.mult)
                    last.then_inc(weighed, 1)

                def step(c):
                    n, w, g = c - 4, c - 2, c + 2
                    if w.live:
                        pool.wait_ge(inverted, w.done())
                    if n.live:
                        pool.wait_ge(meaned, n.done())
                        need(pool, lnroot, (n - 1).done())
                        need(pool, normed, (n - 2).done())
                        pool.tensor_tensor(ve[n.slot % 2][:], mv[n.slot % 2][:, 1:2], K.eps[:], ALU.add).then_inc(eased, 1)
                        pool.wait_ge(eased, n.done())
                        pool.tensor_tensor(rs[n.slot % 2][:], ve[n.slot % 2][:], K.half[:, 0:1], ALU.pow).then_inc(lnroot, 1)
                    if w.live:
                        weigh(w, 0)
                    q = c - 7
                    if feed and q.live:
                        need(pool, fmeaned, q.done())
                        need(pool, fnormed, (q - 2).done())
                        pool.tensor_tensor(fve[q.slot % 2][:], fmv[q.slot % 2][:, 1:2], K.eps[:], ALU.add).then_inc(feased, 1)
                        need(pool, feased, q.done())
                        pool.tensor_tensor(frs[q.slot % 2][:], fve[q.slot % 2][:], K.half[:, 0:1], ALU.pow).then_inc(flnroot, 1)
                    if g.live and windowed:
                        pool.wait_ge(squared, g.done(2))
                        need(pool, scaled, (g - 2).done(2))
                        pool.tensor_tensor(rms[g.slot % 2][:], ss[g.slot % 2][:], K.half[:], ALU.pow).then_inc(rooted, 1)
                    if w.live:
                        weigh(w, 1)
                pipeline(pool, step, ring, nseq, *span)
        K.passed(last_pass)


def attend_narrow(K, D, tag, x_dram, out_dram, nseq, cross):
    nc = K.nc
    units = 4 if cross else 2
    ring, uring, ucount = 4, 4 * units, nseq * units
    per_unit = NH // units
    wide = 1024 // per_unit
    keys = P + CTX if cross else P
    chunks = [(0, P), (P, CTX)] if cross else [(0, P)]
    behind = 1 if cross else 2
    gain = HD ** -0.5

    def heads(j):
        return [4 * g + m for m in range(j * per_unit // 4, (j + 1) * per_unit // 4) for g in range(4)]

    def item(u):
        return At(u.p, u.slot // units, ring, nseq)

    def bank(x):
        return not isinstance(x.p, int) or 0 <= x.n < nseq + 2 + behind

    K.taken = 0
    with ExitStack() as ctx:
        def sb(name, shape, dtype=F32):
            return K.sb(tag + name, shape, dtype, ctx)

        def sem(name):
            return K.sem(tag + name)

        x = [sb(f"x{i}", [P, P]) for i in range(ring)]
        fs = [sb(f"fs{i}", [P, P]) for i in range(ring)] if cross else None
        cx = [sb(f"cx{i}", [P, P]) for i in range(ring)] if cross else None
        res = [sb(f"res{i}", [P, P]) for i in range(ring)]
        xT = [sb(f"xT{i}", [P, 2 * P]) for i in range(ring)]
        qk = [sb(f"qk{i}", [P, P + keys]) for i in range(ring)]
        spun = [sb(f"spun{i}", [P, 2 * P]) for i in range(2)]
        Qx = [sb(f"Qx{i}", [P, NH, P]) for i in range(2)]
        Vx = [sb(f"Vx{i}", [P, len(chunks), NH, 32]) for i in range(ring)]
        pr = K.pr
        nmax = [sb(f"nmax{i}", [P, per_unit]) for i in range(4)]
        tot = [sb(f"tot{i}", [P, NH]) for i in range(ring)]
        inv = [sb(f"inv{i}", [P, NH]) for i in range(2)]
        invx = [sb(f"invx{i}", [P, P]) for i in range(2)]
        invT = [sb(f"invT{i}", [P, P]) for i in range(2)]
        oT = [sb(f"oT{i}", [P, P]) for i in range(2)]
        pT = [sb(f"pT{i}", [P, 1024]) for i in range(2)]
        y = [sb(f"y{i}", [P, P]) for i in range(2)]
        yb = [sb(f"yb{i}", [P, P]) for i in range(2)]
        stats = [sb(f"st{i}", [P, 6]) for i in range(2)]
        mv = [sb(f"mv{i}", [P, 2]) for i in range(2)]
        ve = [sb(f"ve{i}", [P, 1]) for i in range(2)]
        rs = [sb(f"rs{i}", [P, 1]) for i in range(2)]
        xo = [sb(f"xo{i}", [P, P]) for i in range(ring)]
        junk = sb("junk", [P, 1])

        x_in = [sem(f"x_in{i}") for i in range(ring)]
        res_in = [sem(f"res_in{i}") for i in range(ring)]
        stored = [sem(f"stored{i}") for i in range(ring)]
        shared_ps, proj_ps, S_ps, pT_ps, O_ps, inv_ps = (sem(n) for n in (
            "shared_ps", "proj_ps", "S_ps", "pT_ps", "O_ps", "inv_ps"))
        shared_sb, proj_sb, invT_sb, oT_sb = (sem(n) for n in ("shared_sb", "proj_sb", "invT_sb", "oT_sb"))
        pT_sb = [sem("pT_sb0"), sem("pT_sb1")]
        exped, halves, maxed, inverted, spread = (sem(n) for n in (
            "exped", "halves", "maxed", "inverted", "spread"))
        joined, summed, counted, meaned, normed = (sem(n) for n in ("joined", "summed", "counted", "meaned", "normed"))
        cleared, masked, eased, lnroot = sem("cleared"), sem("masked"), sem("eased"), sem("lnroot")

        W = K.W
        arrivals = 3 if cross else 1
        span = (-2 * units, 2 * ring * units, (nseq - 3) // ring * ring * units, (nseq + behind + 2) * units)
        wq, wk, wv, wout = (K.xw[:, n, :] for n in range(4)) if cross else (K.rw[:, n, :] for n in (0, 1, 2, 5))

        def turn(t, half, copy):
            cols = slice(512 * half, 512 * half + 512)
            if not cross:
                return copy(pT[t.slot % 2][:, cols], W[half][:])
            w = W[half][:].rearrange("p (n c q) -> p n c q", n=2, c=2)
            d = pT[t.slot % 2][:, cols].rearrange("p (n c q) -> p n c q", n=2, c=2)
            copy(d[:, :, 0, :], w[:, :, 0, :])
            return copy(d[0:CTX, :, 1, :], w[0:CTX, :, 1, :])

        with nc.Block() as block:
            @block.sync
            def _(sp):
                def step(c):
                    a, o = c + 4, c - 4
                    if a.live:
                        need(sp, proj_sb, (a - 4).done())
                        sp.dma_start(x[a.slot][:], x_dram[a.n]).then_inc(x_in[a.slot], 16)
                        if cross:
                            sp.dma_start(fs[a.slot][:], D["fside_BxSxS_0"][a.n]).then_inc(x_in[a.slot], 16)
                            sp.dma_start(cx[a.slot][0:CTX, :], D["ctx_1024"][a.n]).then_inc(x_in[a.slot], 16)
                    if c.live:
                        need(sp, summed, (c - 4).done())
                        sp.dma_start(res[c.slot][:], x_dram[c.n]).then_inc(res_in[c.slot], 16)
                    if o.live:
                        need(sp, normed, o.done())
                        sp.dma_start(out_dram[o.n], xo[o.slot][:]).then_inc(stored[o.slot], 16)
                pipeline(sp, step, ring, nseq, -4, 4, (nseq - 4) // ring * ring, nseq + 4)
                for i in range(ring):
                    sp.wait_ge(stored[i], 16 * len(range(i, nseq, ring)))

            @block.tensor
            def _(pe):
                pe.wait_ge(cleared, ring)

                def turn_sums(r):
                    if r.live and r.slot % units == units - 1:
                        k = item(r)
                        need(pe, spread, k.done())
                        pe.transpose(W[3][:, P:2 * P], invx[k.slot % 2][:], K.ident[:]).then_inc(inv_ps, 1)

                def step(u):
                    t, j, i = u - 2, u.slot % units, item(u)
                    b, a = i + 1, i + 2
                    if t.live:
                        need(pe, exped, t.done())
                        for half in range(2):
                            need(pe, pT_sb[half], (t - 1).done())
                            for n in range(4 * half, 4 * half + 4):
                                at, size = (wide * (n // 2) + chunks[n % 2][0], chunks[n % 2][1]) if cross else (n * P, P)
                                last = pe.transpose(W[half][0:size, (n % 4) * P:(n % 4 + 1) * P],
                                                    pr[t.slot % 4][:, at:at + size], K.ident[:])
                            last.then_inc(pT_ps, 1)
                    if j == 0 and b.live:
                        need(pe, shared_sb, b.done())
                        if cross:
                            pe.matmul(W[2][:, 0:P], wq, xT[b.slot][:, 0:P], start=True, stop=True)
                            pe.matmul(W[2][:, P:2 * P], wk, xT[b.slot][:, P:2 * P], start=True, stop=True)
                            last = pe.matmul(W[2][:, 2 * P:3 * P], xT[b.slot][:, P:2 * P], wv, start=True, stop=True)
                        else:
                            for n, w in enumerate((wq, wk, K.rw[:, 3, :], K.rw[:, 4, :])):
                                last = pe.matmul(W[2][:, n * P:(n + 1) * P], w, xT[b.slot][:, 0:P], start=True, stop=True)
                        last.then_inc(proj_ps, 1)
                    if j == units - 1 and bank(a):
                        o = i + (-behind)
                        last = None
                        if b.live:
                            need(pe, proj_sb, b.done())
                        else:
                            need(pe, shared_sb, (a - 1).done())
                        if o.live:
                            need(pe, oT_sb, o.done())
                            last = pe.matmul(W[2][:, 0:P], oT[o.slot % 2][:], wout, start=True, stop=True)
                        if not cross and b.live:
                            last = pe.matmul(W[2][:, P:2 * P], xT[b.slot][:, 0:P], wv, start=True, stop=True)
                        if a.live:
                            need(pe, x_in[a.slot], a.p * (16 * arrivals) + 16 * arrivals)
                            if cross:
                                pe.transpose(W[2][:, 2 * P:3 * P], fs[a.slot][:], K.ident[:])
                                pe.transpose(W[2][:, 3 * P:3 * P + CTX], cx[a.slot][0:CTX, :], K.ident[0:CTX, 0:CTX])
                                last = pe.transpose(W[2][:, P:2 * P], x[a.slot][:], K.ident[:])
                            else:
                                last = pe.transpose(W[2][:, 2 * P:3 * P], x[a.slot][:], K.ident[:])
                        last.then_inc(shared_ps, 1)
                    if u.live:
                        need(pe, masked, u.done())
                        need(pe, exped, (u - 2).done())
                        if not cross:
                            for half in range(2):
                                pe.matmul(K.S[u.slot % 2][:, 512 * half:512 * half + 512], K.identb[:], K.causal[:],
                                          start=True, stop=False)
                        for n, h in enumerate(heads(j)):
                            if n == 1:
                                turn_sums(u - 3)
                            last = pe.matmul(K.S[u.slot % 2][:, n * wide:n * wide + keys], Qx[i.slot % 2][:, h, :],
                                             qk[i.slot][:, P:P + keys], start=cross,
                                             stop=cross or n % 4 == 3)
                        last.then_inc(S_ps, 1)
                    else:
                        turn_sums(u - 3)
                    if t.live:
                        k, tj = item(t), t.slot % units
                        need(pe, pT_sb[0], t.done())
                        need(pe, pT_sb[1], t.done())
                        need(pe, oT_sb, (k - 1).done())
                        for n in range(8):
                            h, c = (heads(tj)[n // 2], n % 2) if cross else (heads(tj)[n], 0)
                            first = tj == 0 and (n % 2 == 0 if cross else n < 4)
                            final = tj == units - 1 and (n % 2 == 1 if cross else n >= 4)
                            size = chunks[c][1]
                            g = h // 4
                            last = pe.matmul(W[3][32 * g:32 * g + 32, 0:P], Vx[k.slot][0:size, c, h, :],
                                             pT[t.slot % 2][0:size, n * P:(n + 1) * P], start=first, stop=final)
                        last.then_inc(O_ps, 1)
                pipeline(pe, step, uring, ucount, *span)

            @block.scalar
            def _(act):
                def step(u):
                    e, t = u - 1, u - 2
                    if e.live:
                        need(act, maxed, e.done())
                        need(act, pT_ps, (e - 4).done(2))
                        k = item(e)
                        need(act, inverted, (k - 4).done())
                    for n, h in enumerate(heads((u.slot - 1) % units)):
                        if t.live and n == (1 if cross else 2):
                            need(act, O_ps, (t - 2).done())
                            need(act, pT_ps, t.done(2))
                            turn(t, 1, act.copy).then_inc(pT_sb[1], 1)
                        if e.live:
                            cols = slice(n * wide, n * wide + keys)
                            last = act.activation(pr[e.slot % 4][:, cols], K.S[e.slot % 2][:, cols], ACT.Exp,
                                                  bias=nmax[e.slot % 4][:, n:n + 1], accum_out=tot[k.slot][:, h:h + 1])
                    if e.live:
                        last.then_inc(exped, 1)
                pipeline(act, step, uring, ucount, *span)

            @block.vector
            def _(dve):
                for i in range(ring):
                    dve.memset(Vx[i][:], 0.0).then_inc(cleared, 1)
                dve.wait_ge(cleared, ring)

                def put(slot, c, size, src, bias):
                    v = Vx[slot][0:size, c, :, :]
                    for m in range(4):
                        dst = v[:, m:NH:4, HD * m:HD * m + HD]
                        s = src.rearrange("p (g m d) -> p m g d", g=4, m=4)[:, m]
                        if bias is None:
                            last = dve.tensor_copy(dst, s)
                        else:
                            last = dve.tensor_tensor(dst, s, bias.rearrange("p (g m d) -> p m g d", g=4, m=4)[:, m], ALU.add)
                    return last

                def step(u):
                    t, j, i = u - 2, u.slot % units, item(u)
                    b, a = i + 1, i + 2
                    if t.live:
                        need(dve, O_ps, (t - 2).done())
                        need(dve, pT_ps, t.done(2, 1))
                        turn(t, 0, dve.tensor_copy).then_inc(pT_sb[0], 1)
                    if j == 0:
                        if b.live:
                            need(dve, proj_ps, b.done())
                            need(dve, S_ps, (b - 4).done(units))
                            need(dve, masked, (b - 4).done(units))
                            if cross:
                                dve.tensor_scalar(qk[b.slot][:, 0:P], W[2][:, 0:P], K.xb[:, 0:1], gain, ALU.add, ALU.mult)
                                dve.tensor_scalar(qk[b.slot][:, P:2 * P], W[2][:, P:2 * P], K.xb[:, 1:2], None, ALU.add)
                                need(dve, O_ps, (b - 4).done(units))
                                put(b.slot, 1, CTX, cx[b.slot][0:CTX, :], None)
                                put(b.slot, 0, P, W[2][:, 2 * P:3 * P], K.rowb[:, 0, :]).then_inc(proj_sb, 1)
                            else:
                                for s in range(2):
                                    dve.tensor_tensor(spun[s][:], W[2][:, 2 * s * P:2 * (s + 1) * P],
                                                      K.rope[:, 2 * s * P:2 * (s + 1) * P], ALU.mult).then_inc(halves, 1)
                                dve.wait_ge(halves, b.done(2))
                                dve.tensor_tensor(qk[b.slot][:], spun[0][:], spun[1][:], ALU.add).then_inc(proj_sb, 1)
                    r = u - 3
                    if r.live and r.slot % units == units - 1:
                        k = item(r)
                        need(dve, inv_ps, k.done())
                        dve.tensor_copy(invT[k.slot % 2][:], W[3][:, P:2 * P]).then_inc(invT_sb, 1)
                        need(dve, shared_ps, (k + behind).done())
                        need(dve, invT_sb, k.done())
                        dve.tensor_tensor(oT[k.slot % 2][:], W[3][:, 0:P], invT[k.slot % 2][:], ALU.mult).then_inc(oT_sb, 1)
                    if j == units - 1 and bank(a):
                        need(dve, shared_ps, a.done())
                        o = i + (-behind)
                        if o.live:
                            need(dve, res_in[o.slot], o.landed())
                            need(dve, normed, (o - 2).done())
                            if cross:
                                dve.tensor_tensor(yb[o.slot % 2][:], res[o.slot][:], K.rowb[:, 1, :], ALU.add).then_inc(joined, 1)
                                need(dve, joined, o.done())
                            dve.tensor_tensor(y[o.slot % 2][:], W[2][:, 0:P], (yb[o.slot % 2] if cross else res[o.slot])[:],
                                              ALU.add).then_inc(summed, 1)
                            need(dve, summed, o.done())
                            dve.bn_stats(stats[o.slot % 2][:], y[o.slot % 2][:]).then_inc(counted, 1)
                        if not cross and b.live:
                            need(dve, O_ps, (b - 4).done(units))
                            put(b.slot, 0, P, W[2][:, P:2 * P], None)
                        if o.live:
                            need(dve, counted, o.done())
                        if a.live:
                            if cross:
                                need(dve, S_ps, (a - 4).done(units))
                                dve.tensor_copy(qk[a.slot][:, 2 * P:2 * P + CTX], W[2][:, 3 * P:3 * P + CTX])
                                dve.tensor_copy(xT[a.slot][:], W[2][:, P:3 * P]).then_inc(shared_sb, 1)
                            else:
                                dve.tensor_copy(xT[a.slot][:, 0:P], W[2][:, 2 * P:3 * P]).then_inc(shared_sb, 1)
                        else:
                            dve.tensor_copy(junk[:], K.half[:, 0:1]).then_inc(shared_sb, 1)
                        if o.live:
                            dve.bn_aggr(mv[o.slot % 2][:], stats[o.slot % 2][:]).then_inc(meaned, 1)
                    if u.live:
                        need(dve, S_ps, u.done())
                        need(dve, exped, (u - 4).done())
                        src = K.S[u.slot % 2][:].rearrange("p (n k) -> p n k", k=wide)
                        dve.tensor_reduce(nmax[u.slot % 4][:], src[:, :, 0:keys], AX.X, ALU.max, negate=True).then_inc(maxed, 1)
                    if j == 0:
                        n = i + (-1 - behind)
                        if n.live:
                            need(dve, lnroot, n.done())
                            need(dve, stored[n.slot], (n - 4).landed())
                            dve.tensor_scalar(xo[n.slot][:], y[n.slot % 2][:], mv[n.slot % 2][:, 0:1], rs[n.slot % 2][:, 0:1],
                                              ALU.subtract, ALU.mult).then_inc(normed, 1)
                    v = u - 2
                    if v.live and v.slot % units == units - 1:
                        k = item(v)
                        need(dve, exped, v.done())
                        dve.reciprocal(inv[k.slot % 2][:], tot[k.slot][:]).then_inc(inverted, 1)
                        need(dve, inverted, k.done())
                        need(dve, inv_ps, (k - 2).done())
                        dve.tensor_copy(invx[k.slot % 2][:].rearrange("p (h d) -> p h d", h=NH),
                                        inv[k.slot % 2][:].rearrange("p (h a) -> p h a", a=1).to_broadcast([P, NH, HD])
                                        ).then_inc(spread, 1)
                pipeline(dve, step, uring, ucount, *span)

            @block.gpsimd
            def _(pool):
                K.clear(pool)

                def step(u):
                    j, i = u.slot % units, item(u)
                    b, n = i + 1, i + (-1 - behind)
                    if j == 0 and b.live:
                        need(pool, proj_sb, b.done())
                        need(pool, S_ps, (b - 2).done(units))
                    if j == 0 and n.live:
                        need(pool, meaned, n.done())
                        need(pool, normed, (n - 2).done())
                        pool.tensor_tensor(ve[n.slot % 2][:], mv[n.slot % 2][:, 1:2], K.eps[:], ALU.add).then_inc(eased, 1)
                        need(pool, eased, n.done())
                        pool.tensor_tensor(rs[n.slot % 2][:], ve[n.slot % 2][:], K.half[:, 0:1], ALU.pow).then_inc(lnroot, 1)
                    if b.live:
                        for h in heads(j):
                            last = pool.tensor_scalar(Qx[b.slot % 2][:, h, :], qk[b.slot][:, 0:P], K.headmask[:, h:h + 1],
                                                      1.0, ALU.mult, ALU.mult)
                        last.then_inc(masked, 1)
                pipeline(pool, step, uring, ucount, *span)
        K.passed()


def experts(K, D, tag, x_dram, out_dram, nseq):
    nc = K.nc
    units, T = EXPERTS + 1, 2 * P
    ring, count = 2, nseq // 2
    uring, ucount = ring * units, count * units
    x_pairs = x_dram.rearrange("(i a) p d -> i p a d", a=2)
    out_pairs = out_dram.rearrange("(i a) p d -> i p a d", a=2)

    def item(u):
        return At(u.p, u.slot // units, ring, count)

    K.taken = 0
    with ExitStack() as ctx:
        def sb(name, shape, dtype=F32):
            return K.sb(tag + name, shape, dtype, ctx)

        def sem(name):
            return K.sem(tag + name)

        x = [sb(f"x{i}", [P, 2, P]) for i in range(2)]
        xT = [sb(f"xT{i}", [P, T]) for i in range(2)]
        th = [sb(f"th{i}", [P, 2 * T]) for i in range(2)]
        gh = sb("gh", [P, 2 * T])
        gu = [sb(f"gu{i}", [P, 2, T]) for i in range(2)]
        acc = [sb(f"acc{i}", [P, 2, P]) for i in range(2)]
        best = [sb(f"best{i}", [P, 2, EXPERTS]) for i in range(2)]
        at = [sb(f"at{i}", [P, 2, EXPERTS], U32) for i in range(2)]
        atf = [sb(f"atf{i}", [P, 2, 2]) for i in range(2)]
        gap = [sb(f"gap{i}", [P, 2]) for i in range(2)]
        ex = [sb(f"ex{i}", [P, 2]) for i in range(2)]
        den = [sb(f"den{i}", [P, 2]) for i in range(2)]
        prob = [sb(f"prob{i}", [P, 2, 2]) for i in range(2)]
        part = [sb(f"part{i}", [P, 2, EXPERTS]) for i in range(2)]
        we = [sb(f"we{i}", [P, 2, EXPERTS]) for i in range(2)]
        logits = [sb(f"logits{i}", [P, 2, EXPERTS]) for i in range(2)]
        stats = [sb(f"st{i}", [P, 2, 6]) for i in range(2)]
        mv = [sb(f"mv{i}", [P, 2, 2]) for i in range(2)]
        ve = [sb(f"ve{i}", [P, 2]) for i in range(2)]
        rs = [sb(f"rs{i}", [P, 2]) for i in range(2)]
        xo = [sb(f"xo{i}", [P, 2, P]) for i in range(2)]

        x_in = [sem(f"x_in{i}") for i in range(2)]
        stored = [sem(f"stored{i}") for i in range(2)]
        xT_ps, gate_ps, h_ps, hu_ps, out_ps = sem("xT_ps"), sem("gate_ps"), sem("h_ps"), sem("hu_ps"), sem("out_ps")
        xT_sb, tanhed, opened, gated, added = sem("xT_sb"), sem("tanhed"), sem("opened"), sem("gated"), sem("added")
        picked, exped, weights = sem("picked"), sem("exped"), sem("weights")
        counted, meaned, eased, lnroot, normed = sem("counted"), sem("meaned"), sem("eased"), sem("lnroot"), sem("normed")

        W = K.W
        span = (-units, 2 * uring, (count - 1) // ring * ring * units, ucount + units)

        with nc.Block() as block:
            @block.sync
            def _(sp):
                def step(c):
                    a, o = c + 2, c - 2
                    if o.live:
                        need(sp, normed, o.done(2))
                        sp.dma_start(out_pairs[o.n], xo[o.slot][:]).then_inc(stored[o.slot], 16)
                    if a.live:
                        need(sp, added, (a - 2).done(2 * units, 2))
                        sp.dma_start(x[a.slot][:], x_pairs[a.n]).then_inc(x_in[a.slot], 16)
                pipeline(sp, step, ring, count, -2, 2, (count - 2) // ring * ring, count + 2)
                for i in range(ring):
                    sp.wait_ge(stored[i], 16 * len(range(i, count, ring)))

            @block.tensor
            def _(pe):
                pe.wait_ge(K.experts_in, K.EXPERTS_IN)
                def step(u):
                    j, i, t = u.slot % units, item(u), u - 2
                    b = i + 1
                    if u.live:
                        need(pe, xT_sb, i.done())
                        for w, at0, read, signal in ((K.e1, 0, opened, h_ps), (K.e2, 512, gated, hu_ps)):
                            need(pe, read, (u - 2).done())
                            for blk in range(2):
                                last = pe.matmul(K.S[u.slot % 2][:, at0 + blk * T:at0 + (blk + 1) * T],
                                                 w[:, j, blk * P:(blk + 1) * P], xT[i.slot][:], start=True, stop=True)
                            last.then_inc(signal, 1)
                    if t.live:
                        need(pe, gated, t.done())
                        need(pe, added, (t - 2).done(2))
                        e = t.slot % units
                        for half in range(2):
                            for blk in range(2):
                                last = pe.matmul(W[t.slot % 2][:, half * P:(half + 1) * P],
                                                 gu[t.slot % 2][:, blk, half * P:(half + 1) * P], K.e3[:, e, blk, :],
                                                 start=(blk == 0), stop=(blk == 1))
                        last.then_inc(out_ps, 1)
                    if b.live and j == 1:
                        need(pe, x_in[b.slot], b.landed())
                        need(pe, picked, (b - 1).done(3))
                        pe.transpose(W[2][:, 0:P], x[b.slot][:, 0, :], K.ident[:])
                        pe.transpose(W[2][:, P:T], x[b.slot][:, 1, :], K.ident[:]).then_inc(xT_ps, 1)
                    if b.live and j == 2:
                        need(pe, xT_sb, b.done())
                        for half in range(2):
                            last = pe.matmul(W[2][:, T + half * EXPERTS:T + (half + 1) * EXPERTS],
                                             xT[b.slot][:, half * P:(half + 1) * P], K.gate[:], start=True, stop=True)
                        last.then_inc(gate_ps, 1)
                pipeline(pe, step, uring, ucount, *span)

            @block.scalar
            def _(act):
                def step(u):
                    j, i = u.slot % units, item(u)
                    b = i + 1
                    if u.live:
                        need(act, h_ps, u.done())
                        need(act, opened, (u - 2).done())
                        act.activation(th[u.slot % 2][:], K.S[u.slot % 2][:, 0:2 * T], ACT.Tanh, scale=0.5).then_inc(tanhed, 1)
                    if b.live and j == 3:
                        need(act, picked, b.done(3, 2))
                        need(act, weights, (b - 2).done(10))
                        act.activation(ex[b.slot][:], gap[b.slot][:], ACT.Exp).then_inc(exped, 1)
                pipeline(act, step, uring, ucount, *span)

            @block.vector
            def _(dve):
                def choose(b):
                    need(dve, gate_ps, b.done())
                    need(dve, weights, (b - 2).done(10))
                    need(dve, exped, (b - 2).done())
                    dve.tensor_copy(logits[b.slot][:], W[2][:, T:T + 2 * EXPERTS].rearrange("p (a e) -> p a e", a=2))
                    for half in range(2):
                        last = dve.max(best[b.slot][:, half, :], W[2][:, T + half * EXPERTS:T + (half + 1) * EXPERTS])
                    last.then_inc(picked, 1)
                    dve.wait_ge(picked, b.done(3, 1))
                    dve.tensor_tensor(gap[b.slot][:], best[b.slot][:, :, 1], best[b.slot][:, :, 0],
                                      ALU.subtract).then_inc(picked, 1)

                def name_chosen(b):
                    for half in range(2):
                        last = dve.max_index(at[b.slot][:, half, :], best[b.slot][:, half, :],
                                             W[2][:, T + half * EXPERTS:T + (half + 1) * EXPERTS])
                    last.then_inc(picked, 1)

                def weigh(b, stage):
                    s = b.slot
                    if stage == 0:
                        softmax(b, s)
                    elif stage == 1:
                        dve.wait_ge(weights, b.done(10, 4))
                        for half in range(2):
                            for n, dst in enumerate((part, we)):
                                dve.tensor_scalar(dst[s][:, half, :], K.iota[:], atf[s][:, half, n:n + 1],
                                                  prob[s][:, half, n:n + 1], ALU.is_equal, ALU.mult).then_inc(weights, 1)
                    else:
                        dve.wait_ge(weights, b.done(10, 8))
                        for half in range(2):
                            dve.tensor_tensor(we[s][:, half, :], we[s][:, half, :], part[s][:, half, :],
                                              ALU.add).then_inc(weights, 1)

                def softmax(b, s):
                    need(dve, exped, b.done())
                    need(dve, picked, b.done(3))
                    need(dve, added, (b - 2).done(2 * units))
                    dve.tensor_scalar(den[s][:], ex[s][:], 2.0, 2.0, ALU.mult, ALU.add).then_inc(weights, 1)
                    dve.tensor_copy(atf[s][:], at[s][:, :, 0:2]).then_inc(weights, 1)
                    dve.wait_ge(weights, b.done(10, 1))
                    dve.reciprocal(prob[s][:, :, 0], den[s][:]).then_inc(weights, 1)
                    dve.wait_ge(weights, b.done(10, 3))
                    dve.tensor_tensor(prob[s][:, :, 1], prob[s][:, :, 0], ex[s][:], ALU.mult).then_inc(weights, 1)

                def step(u):
                    j, i = u.slot % units, item(u)
                    b, t, g = i + 1, u - 3, u - 1
                    k = i - 1
                    if k.live and j == 3:
                        need(dve, added, k.done(2 * units))
                        for half in range(2):
                            last = dve.bn_stats(stats[k.slot][:, half, :], acc[k.slot][:, half, :])
                        last.then_inc(counted, 1)
                        need(dve, counted, k.done())
                    if t.live:
                        m, e = item(t), t.slot % units
                        need(dve, out_ps, t.done())
                        need(dve, weights, m.done(10))
                        if e == 0:
                            need(dve, normed, (m - 2).done(2))
                            need(dve, x_in[m.slot], m.landed())
                        else:
                            need(dve, added, (t - 1).done(2))
                        for half in range(2):
                            dve.scalar_tensor_tensor(
                                out=acc[m.slot][:, half, :], in0=W[t.slot % 2][:, half * P:(half + 1) * P],
                                scalar=0.5 if e == EXPERTS else we[m.slot][:, half, e:e + 1],
                                in1=(x if e == 0 else acc)[m.slot][:, half, :], op0=ALU.mult, op1=ALU.add).then_inc(added, 1)
                    if g.live:
                        need(dve, tanhed, g.done())
                        need(dve, gated, (g - 1).done())
                        dve.scalar_tensor_tensor(out=gh[:], in0=th[g.slot % 2][:], scalar=1.0, in1=K.S[g.slot % 2][:, 0:2 * T],
                                                 op0=ALU.add, op1=ALU.mult).then_inc(opened, 1)
                        need(dve, opened, g.done())
                        need(dve, hu_ps, g.done())
                        need(dve, out_ps, (g - 2).done())
                        dve.tensor_tensor(gu[g.slot % 2][:].rearrange("p b t -> p (b t)"), gh[:],
                                          K.S[g.slot % 2][:, 2 * T:4 * T], ALU.mult).then_inc(gated, 1)
                    if k.live and j == 3:
                        if not t.live and not g.live:
                            need(dve, counted, k.done())
                        for half in range(2):
                            last = dve.bn_aggr(mv[k.slot][:, half, :], stats[k.slot][:, half, :])
                        last.then_inc(meaned, 1)
                    if b.live and j == 1:
                        need(dve, xT_ps, b.done())
                        need(dve, hu_ps, (b - 2).done(units))
                        dve.tensor_copy(xT[b.slot][:], W[2][:, 0:T]).then_inc(xT_sb, 1)
                    if k.live and j == 8:
                        need(dve, lnroot, k.done())
                        need(dve, stored[k.slot], (k - 2).landed())
                        for half in range(2):
                            dve.tensor_scalar(xo[k.slot][:, half, :], acc[k.slot][:, half, :], mv[k.slot][:, half, 0:1],
                                              rs[k.slot][:, half:half + 1], ALU.subtract, ALU.mult).then_inc(normed, 1)
                    if b.live and j == 2:
                        choose(b)
                    if b.live and j == 4:
                        name_chosen(b)
                    if b.live and 5 <= j < 8:
                        weigh(b, j - 5)
                pipeline(dve, step, uring, ucount, *span)

            @block.gpsimd
            def _(pool):
                K.clear(pool)

                def step(k):
                    if k.live:
                        need(pool, meaned, k.done())
                        need(pool, normed, (k - 2).done(2))
                        pool.tensor_tensor(ve[k.slot][:], mv[k.slot][:, :, 1], K.eps[:].to_broadcast([P, 2]),
                                           ALU.add).then_inc(eased, 1)
                        need(pool, eased, k.done())
                        pool.tensor_tensor(rs[k.slot][:], ve[k.slot][:], K.half[:], ALU.pow).then_inc(lnroot, 1)
                pipeline(pool, step, ring, count, 0, 2, count // ring * ring, count)
        K.passed()


def constants():
    f = np.float32
    q, k = np.arange(P)[:, None], np.arange(P)[None, :]
    rel = k - q
    slopes = np.array([2.0 ** -h for h in range(WH)], f)
    alibi = np.where((rel > 0) | (rel < -16), f(-1e9), slopes[:, None, None] * rel.astype(f)).astype(f)
    inv_freq = (1.0 / 10000.0 ** (np.arange(0, HD, 2, dtype=f) / f(HD))).astype(f)
    freqs = (np.arange(P, dtype=f)[:, None] * inv_freq[None, :]).astype(f)
    spin = [np.tile(fn(freqs).astype(f).T, (2 * NH, 1)) for fn in (np.cos, np.sin)]
    gain = f(HD ** -0.5)
    return {
        "c_ident": np.eye(P, dtype=f),
        "c_alibi": np.ascontiguousarray(alibi.transpose(1, 0, 2).reshape(P, WH * P)),
        "c_iota": np.tile(np.arange(EXPERTS, dtype=f), (P, 1)),
        "c_causal": np.where(rel > 0, f(-255 * 2.0 ** 120), f(0)).astype(f),
        "c_headmask": (np.arange(P)[:, None] // HD == np.arange(NH)[None, :]).astype(f),
        "c_rope": np.ascontiguousarray(np.concatenate([spin[0] * gain, spin[0], spin[1] * gain, spin[1]], 1)),
    }


def build(nc, D, out, nseq):
    with ExitStack() as ctx:
        K = Core(nc, ctx)
        allocate(K)
        set_up(K, D)
        mid = [nc.dram_tensor(f"between{i}", [nseq, P, P], F32, kind="Internal").ap() for i in range(4)]
        attend_wide(K, D, "self0_", D["x"], mid[0], nseq, windowed=True)
        attend_narrow(K, D, "cross0_", mid[0], mid[1], nseq, cross=True)
        experts(K, D, "experts_", mid[1], mid[2], nseq)
        attend_narrow(K, D, "self1_", mid[2], mid[3], nseq, cross=False)
        attend_wide(K, D, "cross1_", mid[3], out, nseq, windowed=False, last_pass=True)


def kernel(**inputs):
    import concourse.bacc as bacc
    from concourse.bass_utils import run_bass_kernel_spmd

    arrays = {name: np.ascontiguousarray(a) for name, a in inputs.items()}
    arrays.update(constants())
    nc = bacc.Bacc("TRN2", target_bir_lowering=False, num_devices=1)
    D = {name: nc.dram_tensor(f"in_{name}", a.shape, mybir.dt.from_np(a.dtype), kind="ExternalInput").ap()
         for name, a in arrays.items()}
    nseq = arrays["x"].shape[0]
    out = nc.dram_tensor("out", [nseq, P, P], F32, kind="ExternalOutput").ap()
    build(nc, D, out, nseq)
    r = run_bass_kernel_spmd(nc, [{f"in_{name}": a for name, a in arrays.items()}], core_ids=[0])
    return r.results[0]["out"]
```
